# Optimizing a Trainium2 kernel written in Bass

```python
import numpy as np
import jax
import jax.numpy as jnp

def _softmax(x, axis=-1):
    return jax.nn.softmax(x, axis=axis)

def _gelu(x):
    return jax.nn.gelu(x, approximate=True)

def _silu(x):
    return jax.nn.silu(x)

def _sigmoid(x):
    return jax.nn.sigmoid(x)

def _layernorm(x, axis=-1, eps=1e-05):
    m = jnp.mean(x, axis=axis, keepdims=True)
    v = jnp.var(x, axis=axis, keepdims=True)
    return (x - m) / jnp.sqrt(v + eps)

def _scatter_add(tgt, idx, src, axis=0):
    return tgt.at[idx].add(src)

def _segment_sum(src, seg, n):
    return jax.ops.segment_sum(src, seg, n)
kernel_name = 'mk_adj_resnorm_d1_adj_r2_e16536'

def setup_inputs(seed: int=0):
    np.random.seed(seed)
    _w = jnp.asarray

    def _rec_inputs():
        import jax
        import jax.numpy as jnp
        _gk = jax.random.key(seed)
        x = -0.0002928 + 1 * jax.random.normal(jax.random.fold_in(_gk, 1), (2048, 256), jnp.float32)
        _a = jax.random.bernoulli(jax.random.fold_in(_gk, 2), 0.00390625, (2048, 2048))
        _a = jnp.logical_or(_a, jnp.swapaxes(_a, -1, -2))
        _a = jnp.logical_or(_a, jnp.eye(2048, dtype=bool))
        _af = _a.astype(jnp.float32)
        adj = _af
        return (x, adj)
    x, adj = _rec_inputs()

    def _L0_gnn_setup():
        import jax, jax.numpy as jnp
        import numpy as np
        N = 4096
        D = 256
        L = 2
        NEG_SLOPE = 0.01

        def _gat_layer(x, W, adj):
            proj = x @ W
            Wh, Ws = jnp.split(proj, 2, axis=-1)
            scores = Wh @ Ws.T
            a = jax.nn.softmax(scores, axis=-1) * adj
            out = a @ Wh
            out = out + x
            return jax.nn.leaky_relu(out, NEG_SLOPE)
        key = jax.random.key(seed)
        k1, k2, k3 = jax.random.split(key, 3)
        inputs = jax.random.normal(k1, (N, D), dtype=jnp.float32)
        adj = jax.random.randint(k2, (N, N), 0, 2).astype(jnp.float32)
        W_stack = jax.random.normal(k3, (L, D, 2 * D), dtype=jnp.float32) * (1.0 / np.sqrt(D))
        return {'inputs': inputs, 'adj': adj, 'W_stack': W_stack}
    _L0_gnn_all = _L0_gnn_setup()
    _L0_gnn_in = {k: v for k, v in _L0_gnn_all.items() if k in ('W_stack',)}
    del _L0_gnn_all
    return {'x': x, 'adj': adj, 'L0_gnn_W_stack': _L0_gnn_in['W_stack']}

def reference(x, adj, L0_gnn_W_stack):
    import jax
    import jax.numpy as jnp

    def _L0_gnn_ref(inputs, adj, W_stack):
        import jax, jax.numpy as jnp
        import numpy as np
        N = 4096
        D = 256
        L = 2
        NEG_SLOPE = 0.01

        def _gat_layer(x, W, adj):
            proj = x @ W
            Wh, Ws = jnp.split(proj, 2, axis=-1)
            scores = Wh @ Ws.T
            a = jax.nn.softmax(scores, axis=-1) * adj
            out = a @ Wh
            out = out + x
            return jax.nn.leaky_relu(out, NEG_SLOPE)
        x = inputs
        for l in range(W_stack.shape[0]):
            x = _gat_layer(x, W_stack[l], adj)
        return x
    x = _layernorm(x + _L0_gnn_ref(x, adj, L0_gnn_W_stack), axis=-1)
    return x

_drawn_inputs = setup_inputs


def setup_inputs(seed=0):
    import zlib

    import numpy as np

    out = dict(_drawn_inputs(seed))
    spreads = {}
    factors = {}
    for name, (base, spread) in spreads.items():
        noise = np.random.default_rng([zlib.crc32(name.encode()), seed]).standard_normal(out[name].shape)
        drawn = base * np.exp(spread * noise) if base else spread * noise
        out[name] = jnp.asarray(drawn.astype(out[name].dtype))
    for name, factor in factors.items():
        out[name] = (out[name] * factor).astype(out[name].dtype)
    return out
```

```python
from contextlib import ExitStack

import concourse.bass as bass
from concourse import mybir

F32 = mybir.dt.float32
F32R = mybir.dt.float32r
ALU = mybir.AluOpType
ACT = mybir.ActivationFunctionType
AX_X = mybir.AxisListType.X

P = 128
BANK = 512
NEG_SLOPE = 0.01
EPS = 1e-05


def gat_resnorm_kernel(nc: bass.Bass, x: bass.AP, adj: bass.AP, W: bass.AP, out: bass.AP):
    N, D = x.shape
    L = W.shape[0]
    T = N // P
    K = D // P
    C = N // BANK
    Q = C
    JB = BANK // P
    TP_BANKS = 3
    BANK_OF_GROUP = [q % TP_BANKS for q in range(Q)]
    assert K == 2 and C == 4 and T % 2 == 0 and T >= 8 and 2 * D == BANK

    x_dram = x.rearrange("(t p) d -> t p d", p=P)
    adj_dram = adj.rearrange("(t p) n -> t p n", p=P)
    out_dram = out.rearrange("(t p) d -> t p d", p=P)
    w_dram = W.rearrange("l (k p) c -> l p k c", p=P)

    with ExitStack() as ctx:
        def sb(name, shape, dt=F32):
            return ctx.enter_context(nc.sbuf_tensor(name, shape, dt))

        def sem(name):
            return ctx.enter_context(nc.semaphore(name))

        scores = ctx.enter_context(nc.psum_tensor("scores", [P, C, BANK], F32))
        tp = ctx.enter_context(nc.psum_tensor("tp", [P, TP_BANKS, BANK], F32))
        pv = ctx.enter_context(nc.psum_tensor("pv", [P, BANK], F32))

        ident = sb("ident", [P, P])
        w_raw = sb("w_raw", [P, L, K, 2 * D])
        w_hi = sb("w_hi", [P, K, 2 * D], F32R)
        w_lo = sb("w_lo", [P, K, 2 * D], F32R)
        x_all = sb("x_all", [P, L, T, D])
        x_stage = sb("x_stage", [P, 2, D])
        xT_hi = sb("xT_hi", [P, 2, K, P], F32R)
        xT_lo = sb("xT_lo", [P, 2, K, P], F32R)
        proj = sb("proj", [P, 2, 2 * D])
        wh = sb("wh", [P, T, 2 * D], F32R)
        whT = sb("whT", [P, T, K, P])
        whT_hi = sb("whT_hi", [P, 2, K, P], F32R)
        whT_lo = sb("whT_lo", [P, 2, K, P], F32R)
        wsT_hi = sb("wsT_hi", [P, K, N], F32R)
        wsT_lo = sb("wsT_lo", [P, K, N], F32R)
        adj_sb = sb("adj_sb", [P, 2, N])
        probs = sb("probs", [P, 2, N])
        probsT_hi = sb("probsT_hi", [P, Q, BANK], F32R)
        probsT_lo = sb("probsT_lo", [P, Q, BANK], F32R)
        bank_max = sb("bank_max", [P, 2, C])
        neg_max = sb("neg_max", [P, 2])
        row_sum = sb("row_sum", [P, 2])
        inv_sum = sb("inv_sum", [P, 2])
        pv_lo = sb("pv_lo", [P, 2, D])
        pv_res = sb("pv_res", [P, 2, D])
        pv_sum = sb("pv_sum", [P, 2, D])
        x_last = sb("x_last", [P, 2, D])
        resid = sb("resid", [P, 2, D])
        stats = sb("stats", [P, 2, nc.vector.BN_STATS_DIM])
        mean_var = sb("mean_var", [P, 2, 2])
        var_eps = sb("var_eps", [P, 2])
        inv_std = sb("inv_std", [P, 2])
        minus_half = sb("minus_half", [P, 1])
        eps = sb("eps", [P, 1])
        normed = sb("normed", [P, 2, D])

        w_loaded = [sem(f"w_loaded{l}") for l in range(L)]
        x_loaded = [sem("x_loaded0"), sem("x_loaded1")]
        adj_loaded = [sem("adj_loaded0"), sem("adj_loaded1")]
        out_stored = [sem("out_stored0"), sem("out_stored1")]
        consts_ready = sem("consts_ready")
        w_hi_ready = sem("w_hi_ready")
        w_split = sem("w_split")
        x_staged = sem("x_staged")
        xT_ready = sem("xT_ready")
        xT_hi_ready = sem("xT_hi_ready")
        xT_split = sem("xT_split")
        proj_ready = sem("proj_ready")
        proj_copied = sem("proj_copied")
        wh_hi_ready = sem("wh_hi_ready")
        wh_split = sem("wh_split")
        wT_ready = sem("wT_ready")
        wsT_hi_ready = sem("wsT_hi_ready")
        wT_split = sem("wT_split")
        whT_hi_ready = sem("whT_hi_ready")
        whT_split = sem("whT_split")
        scores_ready = sem("scores_ready")
        bank_max_ready = sem("bank_max_ready")
        neg_max_ready = sem("neg_max_ready")
        probs_ready = sem("probs_ready")
        inv_sum_ready = sem("inv_sum_ready")
        masked = sem("masked")
        probsT_ready = sem("probsT_ready")
        probsT_hi_ready = sem("probsT_hi_ready")
        probsT_split = sem("probsT_split")
        pv_ready = sem("pv_ready")
        pv_lo_ready = sem("pv_lo_ready")
        pv_res_ready = sem("pv_res_ready")
        pv_sum_ready = sem("pv_sum_ready")
        x_next_ready = sem("x_next_ready")
        resid_ready = sem("resid_ready")
        stats_ready = sem("stats_ready")
        mean_var_ready = sem("mean_var_ready")
        var_eps_ready = sem("var_eps_ready")
        inv_std_ready = sem("inv_std_ready")
        normed_ready = sem("normed_ready")

        block = ctx.enter_context(nc.Block())

        @block.sync
        def _(sp):
            def load_x(t, b):
                sp.dma_start(x_all[:, 0, t, :], x_dram[t]).then_inc(x_loaded[b], 16)

            def load_adj(t, b):
                sp.dma_start(adj_sb[:, b, :], adj_dram[t]).then_inc(adj_loaded[b], 16)

            def store_out(t, b):
                sp.wait_ge(normed_ready, t + 1)
                sp.dma_start(out_dram[t], normed[:, b, :]).then_inc(out_stored[b], 16)

            load_x(0, 0)
            load_x(1, 1)
            with sp.Fori(1, T // 2) as u:
                for b in range(2):
                    sp.wait_ge(x_staged, 2 * u + b - 1)
                    load_x(2 * u + b, b)
            load_adj(0, 0)
            load_adj(1, 1)
            with sp.Fori(1, T // 2) as u:
                for b in range(2):
                    sp.wait_ge(masked, C * (2 * u + b - 1))
                    load_adj(2 * u + b, b)
            for b in range(2):
                sp.wait_ge(masked, C * (T + b - 1))
                load_adj(b, b)
            for b in range(2):
                sp.wait_ge(masked, C * (T + b + 1))
                load_adj(2 + b, b)
            with sp.Fori(2, T // 2) as u:
                for b in range(2):
                    sp.wait_ge(masked, C * (T + 2 * u + b - 1))
                    load_adj(2 * u + b, b)
                    store_out(2 * u + b - 4, b)
            for t in range(T - 4, T):
                store_out(t, t % 2)
            for b in range(2):
                sp.wait_ge(out_stored[b], 16 * (T // 2))

        @block.gpsimd
        def _(pool):
            nc.gpsimd.memset(ident[:], 0.0).then_inc(consts_ready, 1)
            pool.wait_ge(consts_ready, 1)
            nc.gpsimd.affine_select(out=ident[:], in_=ident[:], compare_op=ALU.not_equal, fill=1.0,
                                    base=0, pattern=[[-1, P]], channel_multiplier=1).then_inc(consts_ready, 1)
            nc.gpsimd.memset(minus_half[:], -0.5).then_inc(consts_ready, 1)
            nc.gpsimd.memset(eps[:], EPS).then_inc(consts_ready, 1)
            pool.wait_ge(consts_ready, 4)

            def stage_x(l, t, b, reuse):
                g = l * T + t
                if l == 0:
                    pool.wait_ge(x_loaded[b], 16 * ((t - b) // 2 + 1) if isinstance(t, int) else 8 * (t - b) + 16)
                else:
                    pool.wait_ge(x_next_ready, t + 1)
                if reuse:
                    pool.wait_ge(xT_ready, g - 1)
                nc.gpsimd.tensor_copy(x_stage[:, b, :], x_all[:, l, t, :]).then_inc(x_staged, 1)

            def add_x(l, t, b):
                g = l * T + t
                pool.wait_ge(pv_lo_ready, g + 1)
                nc.gpsimd.tensor_tensor(pv_res[:, b, :], pv_lo[:, b, :], x_all[:, l, t, :],
                                        ALU.add).then_inc(pv_res_ready, 1)

            def add_resid(t, b, reuse):
                pool.wait_ge(x_next_ready, T * (L - 1) + t + 1)
                if reuse:
                    pool.wait_ge(normed_ready, t - 1)
                nc.gpsimd.tensor_tensor(resid[:, b, :], x_last[:, b, :], x_all[:, 0, t, :],
                                        ALU.add).then_inc(resid_ready, 1)

            def inverse_std(t, b):
                pool.wait_ge(mean_var_ready, t + 1)
                nc.gpsimd.tensor_tensor(var_eps[:, b:b + 1], mean_var[:, b, 1:2], eps[:],
                                        ALU.add).then_inc(var_eps_ready, 1)
                pool.wait_ge(var_eps_ready, t + 1)
                nc.gpsimd.tensor_tensor(inv_std[:, b:b + 1], var_eps[:, b:b + 1], minus_half[:],
                                        ALU.pow).then_inc(inv_std_ready, 1)

            for l in range(L):
                last = l == L - 1
                stage_x(l, 0, 0, l > 0)
                stage_x(l, 1, 1, l > 0)
                with pool.Fori(1, T // 2) as u:
                    for b in range(2):
                        stage_x(l, 2 * u + b, b, True)
                if not last:
                    with pool.Fori(0, T // 2) as u:
                        for b in range(2):
                            add_x(l, 2 * u + b, b)
                else:
                    for t in range(4):
                        add_x(l, t, t % 2)
                        if t:
                            inverse_std(t - 1, 1 - t % 2)
                        add_resid(t, t % 2, t >= 2)
                    with pool.Fori(2, T // 2) as u:
                        for b in range(2):
                            add_x(l, 2 * u + b, b)
                            inverse_std(2 * u + b - 1, 1 - b)
                            add_resid(2 * u + b, b, True)
                    inverse_std(T - 1, 1)

        @block.scalar
        def _(act):
            for l in range(L):
                act.dma_start(w_raw[:, l, :, :], w_dram[l]).then_inc(w_loaded[l], 16)

            def proj_evac(l, t, b, reuse):
                g = l * T + t
                act.wait_ge(proj_ready, g + 1)
                if reuse:
                    act.wait_ge(wT_ready, g - 1)
                    act.wait_ge(wh_split, g - 1)
                nc.scalar.copy(proj[:, b, :], scores[:, b, :]).then_inc(proj_copied, 1)

            def xT_evac(l, t, b, reuse):
                g = l * T + t
                act.wait_ge(xT_ready, g + 1)
                if reuse:
                    act.wait_ge(proj_ready, g - 1)
                nc.scalar.copy(xT_hi[:, b, :, :], tp[:, b, 0:D].rearrange("p (k i) -> p k i", k=K)
                               ).then_inc(xT_hi_ready, 1)

            def wT_evac(l, t, b):
                g = l * T + t
                act.wait_ge(wT_ready, g + 1)
                nc.scalar.copy(wsT_hi[:, :, bass.ts(t, P)],
                               scores[:, 2 + b, D:2 * D].rearrange("p (k i) -> p k i", k=K)
                               ).then_inc(wsT_hi_ready, 1)

            def scale_pv_lo(l, t, b):
                g = l * T + t
                act.wait_ge(pv_ready, g + 1)
                act.wait_ge(inv_sum_ready, g + 1)
                nc.scalar.activation(pv_lo[:, b, :], pv[:, D:2 * D], ACT.Copy,
                                     scale=inv_sum[:, b:b + 1]).then_inc(pv_lo_ready, 1)

            def probsT_round(l, t, q):
                act.wait_ge(probsT_ready, Q * (l * T + t) + q + 1)
                nc.scalar.copy(probsT_hi[:, q, :], tp[:, BANK_OF_GROUP[q], :]).then_inc(probsT_hi_ready, 1)

            def exponentials(l, t, b):
                g = l * T + t
                act.wait_ge(neg_max_ready, g + 1)
                nc.scalar.activation(probs[:, b, :], scores[:, :, :].rearrange("p c n -> p (c n)"), ACT.Exp,
                                     bias=neg_max[:, b:b + 1], accum_out=row_sum[:, b:b + 1]
                                     ).then_inc(probs_ready, 1)

            for l in range(L):
                again = l > 0
                xT_evac(l, 0, 0, again)
                xT_evac(l, 1, 1, again)
                proj_evac(l, 0, 0, again)
                xT_evac(l, 2, 0, True)
                proj_evac(l, 1, 1, again)
                wT_evac(l, 0, 0)
                with act.Fori(1, T // 2 - 1) as u:
                    for b in range(2):
                        xT_evac(l, 2 * u + b + 1, 1 - b, True)
                        proj_evac(l, 2 * u + b, b, True)
                        wT_evac(l, 2 * u + b - 1, 1 - b)
                xT_evac(l, T - 1, 1, True)
                proj_evac(l, T - 2, 0, True)
                wT_evac(l, T - 3, 1)
                proj_evac(l, T - 1, 1, True)
                wT_evac(l, T - 2, 0)
                wT_evac(l, T - 1, 1)

                exponentials(l, 0, 0)
                for q in range(Q):
                    probsT_round(l, 0, q)
                exponentials(l, 1, 1)
                with act.Fori(1, T // 2) as u:
                    for b in range(2):
                        s = 2 * u + b
                        scale_pv_lo(l, s - 2, b)
                        for q in range(Q):
                            probsT_round(l, s - 1, q)
                        exponentials(l, s, b)
                scale_pv_lo(l, T - 2, 0)
                for q in range(Q):
                    probsT_round(l, T - 1, q)
                scale_pv_lo(l, T - 1, 1)

        @block.vector
        def _(dve):
            def split_w(l):
                dve.wait_ge(w_loaded[l], 16)
                if l > 0:
                    dve.wait_ge(proj_ready, l * T)
                nc.vector.tensor_copy(w_hi[:], w_raw[:, l, :, :]).then_inc(w_hi_ready, 1)
                dve.wait_ge(w_hi_ready, l + 1)
                nc.vector.tensor_tensor(w_lo[:], w_raw[:, l, :, :], w_hi[:].bitcast(F32),
                                        ALU.subtract).then_inc(w_split, 1)

            def xT_rest(l, t, b):
                g = l * T + t
                dve.wait_ge(xT_hi_ready, g + 1)
                nc.vector.tensor_tensor(xT_lo[:, b, :, :], tp[:, b, 0:D].rearrange("p (k i) -> p k i", k=K),
                                        xT_hi[:, b, :, :].bitcast(F32), ALU.subtract).then_inc(xT_split, 1)

            def split_wh(l, t, b):
                g = l * T + t
                dve.wait_ge(proj_copied, g + 1)
                nc.vector.tensor_copy(wh[:, t, 0:D], proj[:, b, 0:D]).then_inc(wh_hi_ready, 1)
                dve.wait_ge(wh_hi_ready, g + 1)
                nc.vector.tensor_tensor(wh[:, t, D:2 * D], proj[:, b, 0:D], wh[:, t, 0:D].bitcast(F32),
                                        ALU.subtract).then_inc(wh_split, 1)

            def wT_rest(l, t, b):
                g = l * T + t
                dve.wait_ge(wsT_hi_ready, g + 1)
                halves = scores[:, 2 + b, :].rearrange("p (h k i) -> p h k i", h=2, k=K)
                nc.vector.tensor_copy(whT[:, t, :, :], halves[:, 0])
                nc.vector.tensor_tensor(wsT_lo[:, :, bass.ts(t, P)], halves[:, 1],
                                        wsT_hi[:, :, bass.ts(t, P)].bitcast(F32),
                                        ALU.subtract).then_inc(wT_split, 1)

            def split_whT(l, t, b, reuse):
                g = l * T + t
                if reuse:
                    dve.wait_ge(scores_ready, C * (g - 1))
                nc.vector.tensor_copy(whT_hi[:, b, :, :], whT[:, t, :, :]).then_inc(whT_hi_ready, 1)
                dve.wait_ge(whT_hi_ready, g + 1)
                nc.vector.tensor_tensor(whT_lo[:, b, :, :], whT[:, t, :, :], whT_hi[:, b, :, :].bitcast(F32),
                                        ALU.subtract).then_inc(whT_split, 1)

            def maximum(l, t, b, c):
                dve.wait_ge(scores_ready, C * (l * T + t) + c + 1)
                nc.vector.tensor_reduce(bank_max[:, b, c:c + 1], scores[:, c, :], AX_X,
                                        ALU.max).then_inc(bank_max_ready, 1)

            def negate_max(l, t, b):
                dve.wait_ge(bank_max_ready, C * (l * T + t + 1))
                nc.vector.tensor_reduce(neg_max[:, b:b + 1], bank_max[:, b, :], AX_X, ALU.max,
                                        negate=True).then_inc(neg_max_ready, 1)

            def mask(l, t, b):
                g = l * T + t
                dve.wait_ge(probs_ready, g + 1)
                dve.wait_ge(adj_loaded[b], 8 * (g - b) + 16)
                for c in range(C):
                    cols = slice(c * BANK, (c + 1) * BANK)
                    nc.vector.tensor_tensor(probs[:, b, cols], probs[:, b, cols], adj_sb[:, b, cols],
                                            ALU.mult).then_inc(masked, 1)
                nc.vector.reciprocal(inv_sum[:, b:b + 1], row_sum[:, b:b + 1]).then_inc(inv_sum_ready, 1)

            def probsT_rest(l, t, q):
                dve.wait_ge(probsT_hi_ready, Q * (l * T + t) + q + 1)
                nc.vector.tensor_tensor(probsT_lo[:, q, :], tp[:, BANK_OF_GROUP[q], :],
                                        probsT_hi[:, q, :].bitcast(F32), ALU.subtract
                                        ).then_inc(probsT_split, 1)

            def epilogue(l, t, b, reuse):
                g = l * T + t
                dve.wait_ge(pv_res_ready, g + 1)
                nc.vector.scalar_tensor_tensor(out=pv_sum[:, b, :], in0=pv[:, 0:D], scalar=inv_sum[:, b:b + 1],
                                               in1=pv_res[:, b, :], op0=ALU.mult, op1=ALU.add
                                               ).then_inc(pv_sum_ready, 1)
                dve.wait_ge(pv_sum_ready, g + 1)
                if l < L - 1:
                    dst = x_all[:, l + 1, t, :]
                else:
                    dst = x_last[:, b, :]
                    if reuse:
                        dve.wait_ge(resid_ready, t - 1)
                nc.vector.scalar_tensor_tensor(out=dst, in0=pv_sum[:, b, :], scalar=NEG_SLOPE,
                                               in1=pv_sum[:, b, :], op0=ALU.mult, op1=ALU.max
                                               ).then_inc(x_next_ready, 1)

            def statistics(t, b):
                dve.wait_ge(resid_ready, t + 1)
                nc.vector.bn_stats(stats[:, b, :], resid[:, b, :]).then_inc(stats_ready, 1)

            def aggregate(b):
                nc.vector.bn_aggr(mean_var[:, b, :], stats[:, b, :]).then_inc(mean_var_ready, 1)

            def normalise(t, b, reuse):
                if reuse:
                    dve.wait_ge(out_stored[b], 8 * (t - b))
                dve.wait_ge(inv_std_ready, t + 1)
                nc.vector.tensor_scalar(normed[:, b, :], resid[:, b, :], mean_var[:, b, 0:1],
                                        inv_std[:, b:b + 1], ALU.subtract, ALU.mult).then_inc(normed_ready, 1)

            def step(l, s, b, scoring=True, finish=True, split=True):
                first = isinstance(s, int)
                mask(l, s - 1, 1 - b)
                if l == L - 1 and not (first and s < 3):
                    normalise(s - 3, 1 - b, not (first and s < 5))
                if finish:
                    epilogue(l, s - 2, b, not (first and s < 4))
                if split:
                    split_whT(l, s + 1, 1 - b, True)
                if scoring:
                    for c in range(C - 1):
                        maximum(l, s, b, c)
                probsT_rest(l, s - 1, 0)
                probsT_rest(l, s - 1, 1)
                if scoring:
                    maximum(l, s, b, C - 1)
                    negate_max(l, s, b)
                if l == L - 1 and finish:
                    statistics(s - 2, b)
                    dve.wait_ge(stats_ready, s - 1)
                    probsT_rest(l, s - 1, 2)
                    aggregate(b)
                else:
                    probsT_rest(l, s - 1, 2)
                probsT_rest(l, s - 1, 3)

            split_w(0)
            for l in range(L):
                xT_rest(l, 0, 0)
                xT_rest(l, 1, 1)
                split_wh(l, 0, 0)
                xT_rest(l, 2, 0)
                split_wh(l, 1, 1)
                wT_rest(l, 0, 0)
                with dve.Fori(1, T // 2 - 1) as u:
                    for b in range(2):
                        xT_rest(l, 2 * u + b + 1, 1 - b)
                        split_wh(l, 2 * u + b, b)
                        wT_rest(l, 2 * u + b - 1, 1 - b)
                xT_rest(l, T - 1, 1)
                split_wh(l, T - 2, 0)
                wT_rest(l, T - 3, 1)
                split_whT(l, 0, 0, l > 0)
                split_whT(l, 1, 1, l > 0)
                split_wh(l, T - 1, 1)
                wT_rest(l, T - 2, 0)
                wT_rest(l, T - 1, 1)

                if l < L - 1:
                    split_w(l + 1)
                for c in range(C):
                    maximum(l, 0, 0, c)
                negate_max(l, 0, 0)
                step(l, 1, 1, finish=False)
                for t in range(2, 6):
                    step(l, t, t % 2)
                with dve.Fori(3, T // 2 - 1) as u:
                    for b in range(2):
                        step(l, 2 * u + b, b)
                step(l, T - 2, 0)
                step(l, T - 1, 1, split=False)
                step(l, T, 0, scoring=False, split=False)
                if l == L - 1:
                    normalise(T - 2, 0, True)
                epilogue(l, T - 1, 1, True)
                if l == L - 1:
                    statistics(T - 1, 1)
                    dve.wait_ge(stats_ready, T)
                    aggregate(1)
                    normalise(T - 1, 1, True)

        @block.tensor
        def _(pe):
            def transpose_x(l, t, b, reuse):
                g = l * T + t
                pe.wait_ge(x_staged, g + 1)
                if reuse:
                    pe.wait_ge(xT_split, g - 1)
                for k in range(K):
                    mm = nc.tensor.transpose(tp[:, b, k * P:(k + 1) * P], x_stage[:, b, k * P:(k + 1) * P],
                                             ident[:])
                mm.then_inc(xT_ready, 1)

            def project(l, t, b, reuse):
                g = l * T + t
                pe.wait_ge(xT_split, g + 1)
                if reuse:
                    pe.wait_ge(proj_copied, g - 1)
                for k in range(K):
                    nc.tensor.matmul(scores[:, b, :], xT_hi[:, b, k, :], w_hi[:, k, :],
                                     start=(k == 0), stop=False)
                    nc.tensor.matmul(scores[:, b, :], xT_hi[:, b, k, :], w_lo[:, k, :],
                                     start=False, stop=False)
                    mm = nc.tensor.matmul(scores[:, b, :], xT_lo[:, b, k, :], w_hi[:, k, :],
                                          start=False, stop=(k == K - 1))
                mm.then_inc(proj_ready, 1)

            def transpose_w(l, t, b, reuse):
                g = l * T + t
                pe.wait_ge(proj_copied, g + 1)
                if reuse:
                    pe.wait_ge(wT_split, g - 1)
                for h in range(2 * K):
                    mm = nc.tensor.transpose(scores[:, 2 + b, h * P:(h + 1) * P],
                                             proj[:, b, h * P:(h + 1) * P], ident[:])
                mm.then_inc(wT_ready, 1)

            def score(l, t, b, c):
                for k in range(K):
                    cols = slice(c * BANK, (c + 1) * BANK)
                    nc.tensor.matmul(scores[:, c, :], whT_hi[:, b, k, :], wsT_hi[:, k, cols],
                                     start=(k == 0), stop=False)
                    nc.tensor.matmul(scores[:, c, :], whT_hi[:, b, k, :], wsT_lo[:, k, cols],
                                     start=False, stop=False)
                    mm = nc.tensor.matmul(scores[:, c, :], whT_lo[:, b, k, :], wsT_hi[:, k, cols],
                                          start=False, stop=(k == K - 1))
                mm.then_inc(scores_ready, 1)

            def transpose_probs(l, t, b, q):
                g = l * T + t
                pe.wait_ge(masked, C * g + q + 1)
                bank = BANK_OF_GROUP[q]
                if q >= TP_BANKS:
                    pe.wait_ge(probsT_split, Q * g + q - TP_BANKS + 1)
                elif not (isinstance(t, int) and g == 0):
                    held = max(r for r in range(Q) if BANK_OF_GROUP[r] == bank)
                    pe.wait_ge(probsT_split, Q * (g - 1) + held + 1)
                for j in range(JB):
                    lhs = probs[:, b, (q * JB + j) * P:(q * JB + j + 1) * P]
                    mm = nc.tensor.transpose(tp[:, bank, j * P:(j + 1) * P], lhs, ident[:])
                mm.then_inc(probsT_ready, 1)

            def weigh(l, t, q):
                g = l * T + t
                pe.wait_ge(probsT_split, Q * g + q + 1)
                if q == 0 and not (isinstance(t, int) and g == 0):
                    pe.wait_ge(pv_sum_ready, g)
                for j in range(JB):
                    first, final = q == 0 and j == 0, q == Q - 1 and j == JB - 1
                    rows = q * JB + j
                    hi, lo = (a[:, q, j * P:(j + 1) * P] for a in (probsT_hi, probsT_lo))

                    def with_lo():
                        nc.tensor.matmul(pv[:, 0:D], lo, wh[:, rows, 0:D], start=False, stop=False)

                    if final:
                        with_lo()
                    mm = nc.tensor.matmul(pv[:, :], hi, wh[:, rows, :], start=first, stop=final)
                    if not final:
                        with_lo()
                if q == Q - 1:
                    mm.then_inc(pv_ready, 1)

            def step(l, s, b):
                g = l * T + s
                pe.wait_ge(whT_split, g + 1)
                pe.wait_ge(probs_ready, g)
                for c in range(C - 1):
                    score(l, s, b, c)
                transpose_probs(l, s - 1, 1 - b, 0)
                transpose_probs(l, s - 1, 1 - b, 1)
                score(l, s, b, C - 1)
                value_rest(l, s - 1, 1 - b)

            def value_rest(l, t, b):
                transpose_probs(l, t, b, 2)
                weigh(l, t, 0)
                transpose_probs(l, t, b, 3)
                for q in range(1, Q):
                    weigh(l, t, q)

            pe.wait_ge(consts_ready, 2)
            for l in range(L):
                again = l > 0
                transpose_x(l, 0, 0, again)
                transpose_x(l, 1, 1, again)
                pe.wait_ge(w_split, l + 1)
                project(l, 0, 0, again)
                transpose_x(l, 2, 0, True)
                project(l, 1, 1, again)
                transpose_w(l, 0, 0, again)
                with pe.Fori(1, T // 2 - 1) as u:
                    for b in range(2):
                        transpose_x(l, 2 * u + b + 1, 1 - b, True)
                        project(l, 2 * u + b, b, True)
                        transpose_w(l, 2 * u + b - 1, 1 - b, True)
                transpose_x(l, T - 1, 1, True)
                project(l, T - 2, 0, True)
                transpose_w(l, T - 3, 1, True)
                project(l, T - 1, 1, True)
                transpose_w(l, T - 2, 0, True)
                transpose_w(l, T - 1, 1, True)

                pe.wait_ge(whT_split, l * T + 1)
                pe.wait_ge(wh_split, (l + 1) * T)
                pe.wait_ge(wT_split, (l + 1) * T)
                for c in range(C):
                    score(l, 0, 0, c)
                step(l, 1, 1)
                with pe.Fori(1, T // 2) as u:
                    for b in range(2):
                        step(l, 2 * u + b, b)
                transpose_probs(l, T - 1, 1, 0)
                transpose_probs(l, T - 1, 1, 1)
                value_rest(l, T - 1, 1)


_INS = ['x', 'adj', 'L0_gnn_W_stack']
_OUTS = [((2048, 256), 'float32')]


def kernel(**inputs):
    import numpy as _np
    import concourse.bacc as _bacc
    from concourse import mybir as _mybir
    from concourse.bass_utils import run_bass_kernel_spmd as _run

    nc = _bacc.Bacc("TRN2", target_bir_lowering=False, num_devices=1)
    arrays, args = {}, []
    for name in _INS:
        a = _np.ascontiguousarray(inputs[name])
        arrays[f"in_{name}_dram"] = a
        args.append(nc.dram_tensor(f"in_{name}_dram", a.shape, _mybir.dt.from_np(a.dtype), kind="ExternalInput").ap())
    for i, (shape, dtype) in enumerate(_OUTS):
        dt = _mybir.dt.from_np(_np.dtype(dtype))
        args.append(nc.dram_tensor(f"out_{i}_dram", shape, dt, kind="ExternalOutput").ap())
    gat_resnorm_kernel(nc, *args)
    r = _run(nc, [arrays], core_ids=[0])
    got = tuple(r.results[0][f"out_{i}_dram"] for i in range(len(_OUTS)))
    return got[0]
```

```python
from contextlib import ExitStack

import concourse.bass as bass
from concourse import mybir

F32 = mybir.dt.float32
F32R = mybir.dt.float32r
ALU = mybir.AluOpType
ACT = mybir.ActivationFunctionType
AX_X = mybir.AxisListType.X

P = 128
BANK = 512
NEG_SLOPE = 0.01
EPS = 1e-05


def gat_resnorm_kernel(nc: bass.Bass, x: bass.AP, adj: bass.AP, W: bass.AP, out: bass.AP):
    N, D = x.shape
    L = W.shape[0]
    T = N // P
    K = D // P
    C = N // BANK
    Q = C
    JB = BANK // P
    TPG = T // C
    X_PARTS = [(0, 2), (2, 5), (5, T)]
    TP_BANKS = 3
    BANK_OF_GROUP = [q % TP_BANKS for q in range(Q)]
    assert K == 2 and C == 4 and T % 2 == 0 and T >= 8 and 2 * D == BANK

    x_dram = x.rearrange("(t p) d -> p t d", p=P)
    adj_dram = adj.rearrange("(t p) n -> t p n", p=P)
    out_dram = out.rearrange("(t p) d -> t p d", p=P)
    w_dram = W.rearrange("l (k p) c -> l p k c", p=P)

    with ExitStack() as ctx:
        def sb(name, shape, dt=F32):
            return ctx.enter_context(nc.sbuf_tensor(name, shape, dt))

        def sem(name):
            return ctx.enter_context(nc.semaphore(name))

        scores = ctx.enter_context(nc.psum_tensor("scores", [P, C, BANK], F32))
        tp = ctx.enter_context(nc.psum_tensor("tp", [P, TP_BANKS, BANK], F32))
        pv = ctx.enter_context(nc.psum_tensor("pv", [P, BANK], F32))

        ident = sb("ident", [P, P])
        w_raw = sb("w_raw", [P, L, K, 2 * D])
        wa_hi = sb("wa_hi", [P, L, K, D], F32R)
        wa_lo = sb("wa_lo", [P, L, K, D], F32R)
        m_hi = sb("m_hi", [P, L, K, D], F32R)
        m_lo = sb("m_lo", [P, L, K, D], F32R)
        x_all = sb("x_all", [P, L, T, D])
        x_stage = sb("x_stage", [P, 2, D])
        xT_hi = sb("xT_hi", [P, 2, K, P], F32R)
        xT_lo = sb("xT_lo", [P, 2, K, P], F32R)
        keys_hi = sb("keys_hi", [P, K, N], F32R)
        keys_lo = sb("keys_lo", [P, K, N], F32R)
        wh = sb("wh", [P, T, 2 * D], F32R)
        yT = sb("yT", [P, T, K, P])
        yT_hi = sb("yT_hi", [P, 2, K, P], F32R)
        yT_lo = sb("yT_lo", [P, 2, K, P], F32R)
        adj_sb = sb("adj_sb", [P, 2, N])
        probs = sb("probs", [P, 2, N])
        probsT_hi = sb("probsT_hi", [P, Q, BANK], F32R)
        probsT_lo = sb("probsT_lo", [P, Q, BANK], F32R)
        bank_max = sb("bank_max", [P, 2, C])
        neg_max = sb("neg_max", [P, 2])
        bank_sum = sb("bank_sum", [P, 2, C])
        row_sum = sb("row_sum", [P, 2])
        inv_sum = sb("inv_sum", [P, 2])
        pv_lo = sb("pv_lo", [P, 2, D])
        pv_res = sb("pv_res", [P, 2, D])
        pv_sum = sb("pv_sum", [P, 2, D])
        x_last = sb("x_last", [P, 2, D])
        resid = sb("resid", [P, 2, D])
        stats = sb("stats", [P, 2, nc.vector.BN_STATS_DIM])
        mean_var = sb("mean_var", [P, 2, 2])
        var_eps = sb("var_eps", [P, 2])
        inv_std = sb("inv_std", [P, 2])
        minus_half = sb("minus_half", [P, 1])
        eps = sb("eps", [P, 1])
        normed = sb("normed", [P, 2, D])

        w_loaded = [sem(f"w_loaded{l}") for l in range(L)]
        x_loaded = [sem(f"x_loaded{i}") for i in range(len(X_PARTS))]
        adj_loaded = [sem("adj_loaded0"), sem("adj_loaded1")]
        out_stored = [sem("out_stored0"), sem("out_stored1")]
        consts_ready = sem("consts_ready")
        wa_hi_ready = sem("wa_hi_ready")
        wa_split = sem("wa_split")
        wT_ready = sem("wT_ready")
        wT_hi_ready = sem("wT_hi_ready")
        wT_split = sem("wT_split")
        m_ready = sem("m_ready")
        m_hi_ready = sem("m_hi_ready")
        m_split = sem("m_split")
        x_staged = sem("x_staged")
        xT_ready = sem("xT_ready")
        xT_hi_ready = sem("xT_hi_ready")
        xT_split = sem("xT_split")
        keys_hi_ready = sem("keys_hi_ready")
        keys_lo_ready = sem("keys_lo_ready")
        wh_ready = sem("wh_ready")
        wh_hi_ready = sem("wh_hi_ready")
        wh_split = sem("wh_split")
        y_ready = sem("y_ready")
        y_stored = sem("y_stored")
        yT_hi_ready = sem("yT_hi_ready")
        yT_split = sem("yT_split")
        scores_ready = sem("scores_ready")
        bank_max_ready = sem("bank_max_ready")
        neg_max_ready = sem("neg_max_ready")
        probs_ready = sem("probs_ready")
        row_sum_ready = sem("row_sum_ready")
        inv_sum_ready = sem("inv_sum_ready")
        masked = sem("masked")
        probsT_ready = sem("probsT_ready")
        probsT_hi_ready = sem("probsT_hi_ready")
        probsT_split = sem("probsT_split")
        pv_ready = sem("pv_ready")
        pv_lo_ready = sem("pv_lo_ready")
        pv_res_ready = sem("pv_res_ready")
        pv_sum_ready = sem("pv_sum_ready")
        x_next_ready = sem("x_next_ready")
        resid_ready = sem("resid_ready")
        stats_ready = sem("stats_ready")
        mean_var_ready = sem("mean_var_ready")
        var_eps_ready = sem("var_eps_ready")
        inv_std_ready = sem("inv_std_ready")
        normed_ready = sem("normed_ready")

        def wT(l, h):
            return (a[:, 2 * l + h, :].rearrange("p (m k) -> p m k", m=K) for a in (probsT_hi, probsT_lo))

        wT_bank = [[scores[:, 0, :], scores[:, 1, :]], [tp[:, 2, :], pv[:, :]]]
        m_bank = [scores[:, 0, :], scores[:, 1, :]]
        y_bank = [[tp[:, 0, :], tp[:, 1, :]], [tp[:, 2, :], pv[:, :]]]
        wh_bank = [scores[:, 2, 0:D], scores[:, 3, 0:D]]

        def pv_bank(t):
            return scores[:, 0, :] if isinstance(t, int) and t == T - 1 else pv[:, :]

        def by_k(bank):
            return bank.rearrange("p (k i) -> p k i", k=K)

        block = ctx.enter_context(nc.Block())

        @block.sync
        def _(sp):
            def load_adj(t, b):
                sp.dma_start(adj_sb[:, b, :], adj_dram[t]).then_inc(adj_loaded[b], 16)

            def store_out(t, b):
                sp.wait_ge(normed_ready, t + 1)
                sp.dma_start(out_dram[t], normed[:, b, :]).then_inc(out_stored[b], 16)

            def load_x(i):
                part = slice(*X_PARTS[i])
                sp.dma_start(x_all[:, 0, part, :], x_dram[:, part, :]).then_inc(x_loaded[i], 16)

            def load_w(l):
                sp.dma_start(w_raw[:, l, :, :], w_dram[l]).then_inc(w_loaded[l], 16)

            load_x(0)
            load_w(0)
            load_x(1)
            load_x(2)
            for l in range(1, L):
                load_w(l)
            load_adj(0, 0)
            load_adj(1, 1)
            with sp.Fori(1, T // 2) as u:
                for b in range(2):
                    sp.wait_ge(masked, C * (2 * u + b - 1))
                    load_adj(2 * u + b, b)
            for b in range(2):
                sp.wait_ge(masked, C * (T + b - 1))
                load_adj(b, b)
            for b in range(2):
                sp.wait_ge(masked, C * (T + b + 1))
                load_adj(2 + b, b)
            with sp.Fori(2, T // 2) as u:
                for b in range(2):
                    sp.wait_ge(masked, C * (T + 2 * u + b - 1))
                    load_adj(2 * u + b, b)
                    store_out(2 * u + b - 4, b)
            for t in range(T - 4, T):
                store_out(t, t % 2)
            for b in range(2):
                sp.wait_ge(out_stored[b], 16 * (T // 2))

        @block.gpsimd
        def _(pool):
            nc.gpsimd.memset(ident[:], 0.0).then_inc(consts_ready, 1)
            pool.wait_ge(consts_ready, 1)
            nc.gpsimd.affine_select(out=ident[:], in_=ident[:], compare_op=ALU.not_equal, fill=1.0,
                                    base=0, pattern=[[-1, P]], channel_multiplier=1).then_inc(consts_ready, 1)
            nc.gpsimd.memset(minus_half[:], -0.5).then_inc(consts_ready, 1)
            nc.gpsimd.memset(eps[:], EPS).then_inc(consts_ready, 1)
            pool.wait_ge(consts_ready, 4)

            def copy_keys_lo(l, t, b):
                g = l * T + t
                pool.wait_ge(xT_split, g + 1)
                nc.gpsimd.tensor_copy(keys_lo[:, :, bass.ts(t, P)], xT_lo[:, b, :, :].bitcast(F32)
                                      ).then_inc(keys_lo_ready, 1)

            def add_x(l, t, b):
                g = l * T + t
                pool.wait_ge(pv_lo_ready, g + 1)
                nc.gpsimd.tensor_tensor(pv_res[:, b, :], pv_lo[:, b, :], x_all[:, l, t, :],
                                        ALU.add).then_inc(pv_res_ready, 1)

            def add_resid(t, b, reuse):
                pool.wait_ge(x_next_ready, T * (L - 1) + t + 1)
                if reuse:
                    pool.wait_ge(normed_ready, t - 1)
                nc.gpsimd.tensor_tensor(resid[:, b, :], x_last[:, b, :], x_all[:, 0, t, :],
                                        ALU.add).then_inc(resid_ready, 1)

            def inverse_std(t, b):
                pool.wait_ge(mean_var_ready, t + 1)
                nc.gpsimd.tensor_tensor(var_eps[:, b:b + 1], mean_var[:, b, 1:2], eps[:],
                                        ALU.add).then_inc(var_eps_ready, 1)
                pool.wait_ge(var_eps_ready, t + 1)
                nc.gpsimd.tensor_tensor(inv_std[:, b:b + 1], var_eps[:, b:b + 1], minus_half[:],
                                        ALU.pow).then_inc(inv_std_ready, 1)

            for l in range(L):
                last = l == L - 1
                if l == 0:
                    copy_keys_lo(l, 0, 0)
                copy_keys_lo(l, 1, 1)
                with pool.Fori(1, T // 2) as u:
                    for b in range(2):
                        copy_keys_lo(l, 2 * u + b, b)
                if not last:
                    with pool.Fori(0, T // 2 - 1) as u:
                        for b in range(2):
                            add_x(l, 2 * u + b, b)
                    add_x(l, T - 2, 0)
                    copy_keys_lo(l + 1, 0, 0)
                    add_x(l, T - 1, 1)
                else:
                    for t in range(4):
                        add_x(l, t, t % 2)
                        if t:
                            inverse_std(t - 1, 1 - t % 2)
                        add_resid(t, t % 2, t >= 2)
                    with pool.Fori(2, T // 2) as u:
                        for b in range(2):
                            add_x(l, 2 * u + b, b)
                            inverse_std(2 * u + b - 1, 1 - b)
                            add_resid(2 * u + b, b, True)
                    inverse_std(T - 1, 1)

        @block.scalar
        def _(act):
            def wT_round(l, h):
                act.wait_ge(wT_ready, 2 * l + h + 1)
                hi, _ = wT(l, h)
                nc.scalar.copy(hi, by_k(wT_bank[l][h])).then_inc(wT_hi_ready, 1)

            def m_round(l):
                act.wait_ge(m_ready, l + 1)
                nc.scalar.copy(m_hi[:, l, :, :], by_k(m_bank[l])).then_inc(m_hi_ready, 1)

            def xT_round(l, t, b, reuse):
                g = l * T + t
                act.wait_ge(xT_ready, g + 1)
                if reuse:
                    act.wait_ge(keys_hi_ready, g - 1)
                    act.wait_ge(wh_ready, g - 1)
                nc.scalar.copy(xT_hi[:, b, :, :], by_k(tp[:, b, 0:D])).then_inc(xT_hi_ready, 1)

            def copy_keys_hi(l, t, b):
                act.wait_ge(xT_hi_ready, l * T + t + 1)
                nc.scalar.copy(keys_hi[:, :, bass.ts(t, P)], xT_hi[:, b, :, :].bitcast(F32)
                               ).then_inc(keys_hi_ready, 1)

            def wh_round(l, t, b):
                act.wait_ge(wh_ready, l * T + t + 1)
                nc.scalar.copy(wh[:, t, 0:D], wh_bank[b]).then_inc(wh_hi_ready, 1)

            def scale_pv_lo(l, t, b):
                g = l * T + t
                act.wait_ge(pv_ready, g + 1)
                act.wait_ge(inv_sum_ready, g + 1)
                nc.scalar.activation(pv_lo[:, b, :], pv_bank(t)[:, D:2 * D], ACT.Copy,
                                     scale=inv_sum[:, b:b + 1]).then_inc(pv_lo_ready, 1)

            def probsT_round(l, t, q):
                act.wait_ge(probsT_ready, Q * (l * T + t) + q + 1)
                nc.scalar.copy(probsT_hi[:, q, :], tp[:, BANK_OF_GROUP[q], :]).then_inc(probsT_hi_ready, 1)

            def exponentials(l, t, b):
                g = l * T + t
                act.wait_ge(neg_max_ready, g + 1)
                for c in range(C):
                    nc.scalar.activation(probs[:, b, c * BANK:(c + 1) * BANK], scores[:, c, :], ACT.Exp,
                                         bias=neg_max[:, b:b + 1], accum_out=bank_sum[:, b, c:c + 1]
                                         ).then_inc(probs_ready, 1)

            def first_rounds(l):
                xT_round(l, 0, 0, l > 0)
                xT_round(l, 1, 1, l > 0)

            def keys_step(l, t, b):
                xT_round(l, t + 2, b, True)
                wh_round(l, t, b)
                copy_keys_hi(l, t + 2, b)

            first_rounds(0)
            wT_round(0, 0)
            wT_round(0, 1)
            for l in range(L):
                copy_keys_hi(l, 0, 0)
                copy_keys_hi(l, 1, 1)
                with act.Fori(0, T // 2 - 2) as u:
                    for b in range(2):
                        keys_step(l, 2 * u + b, b)
                if l == 0:
                    for later in range(1, L):
                        wT_round(later, 0)
                        wT_round(later, 1)
                keys_step(l, T - 4, 0)
                if l == 0:
                    m_round(0)
                keys_step(l, T - 3, 1)
                if l == 0:
                    for later in range(1, L):
                        m_round(later)
                wh_round(l, T - 2, 0)
                wh_round(l, T - 1, 1)

                exponentials(l, 0, 0)
                for q in range(Q):
                    probsT_round(l, 0, q)
                exponentials(l, 1, 1)
                with act.Fori(1, T // 2) as u:
                    for b in range(2):
                        s = 2 * u + b
                        scale_pv_lo(l, s - 2, b)
                        for q in range(Q):
                            probsT_round(l, s - 1, q)
                        exponentials(l, s, b)
                probsT_round(l, T - 1, 0)
                probsT_round(l, T - 1, 1)
                scale_pv_lo(l, T - 2, 0)
                probsT_round(l, T - 1, 2)
                probsT_round(l, T - 1, 3)
                if l < L - 1:
                    first_rounds(l + 1)
                scale_pv_lo(l, T - 1, 1)

        @block.vector
        def _(dve):
            def split_wa(l):
                dve.wait_ge(w_loaded[l], 16)
                nc.vector.tensor_copy(wa_hi[:, l, :, :], w_raw[:, l, :, 0:D]).then_inc(wa_hi_ready, 1)
                dve.wait_ge(wa_hi_ready, l + 1)
                nc.vector.tensor_tensor(wa_lo[:, l, :, :], w_raw[:, l, :, 0:D], wa_hi[:, l, :, :].bitcast(F32),
                                        ALU.subtract).then_inc(wa_split, 1)

            def wT_rest(l, h):
                dve.wait_ge(wT_hi_ready, 2 * l + h + 1)
                hi, lo = wT(l, h)
                nc.vector.tensor_tensor(lo, by_k(wT_bank[l][h]), hi.bitcast(F32),
                                        ALU.subtract).then_inc(wT_split, 1)

            def m_rest(l):
                dve.wait_ge(m_hi_ready, l + 1)
                nc.vector.tensor_tensor(m_lo[:, l, :, :], by_k(m_bank[l]), m_hi[:, l, :, :].bitcast(F32),
                                        ALU.subtract).then_inc(m_split, 1)

            def stage_x(l, t, b, reuse):
                if reuse:
                    dve.wait_ge(xT_ready, l * T + t - 1)
                if l > 0:
                    dve.wait_ge(x_next_ready, (l - 1) * T + t + 1)
                nc.vector.tensor_copy(x_stage[:, b, :], x_all[:, l, t, :]).then_inc(x_staged, 1)

            def xT_rest(l, t, b, reuse):
                g = l * T + t
                if reuse:
                    dve.wait_ge(keys_lo_ready, g - 1)
                dve.wait_ge(xT_hi_ready, g + 1)
                nc.vector.tensor_tensor(xT_lo[:, b, :, :], by_k(tp[:, b, 0:D]),
                                        xT_hi[:, b, :, :].bitcast(F32), ALU.subtract).then_inc(xT_split, 1)

            def wh_rest(l, t, b):
                dve.wait_ge(wh_hi_ready, l * T + t + 1)
                nc.vector.tensor_tensor(wh[:, t, D:2 * D], wh_bank[b], wh[:, t, 0:D].bitcast(F32),
                                        ALU.subtract).then_inc(wh_split, 1)

            def store_y(l, n):
                for k in range(K):
                    dve.wait_ge(y_ready, K * (l * C + n) + k + 1)
                    nc.vector.tensor_copy(yT[:, n * TPG:(n + 1) * TPG, k, :],
                                          y_bank[n % 2][k].rearrange("p (t i) -> p t i", t=TPG)
                                          ).then_inc(y_stored, 1)

            def split_y(l, t, b, reuse):
                g = l * T + t
                if reuse:
                    dve.wait_ge(scores_ready, C * (g - 1))
                if isinstance(t, int) and t == 0:
                    dve.wait_ge(y_stored, K * (l * C + 1))
                if isinstance(t, int) and t == TPG:
                    dve.wait_ge(y_stored, K * (l + 1) * C)
                nc.vector.tensor_copy(yT_hi[:, b, :, :], yT[:, t, :, :]).then_inc(yT_hi_ready, 1)
                dve.wait_ge(yT_hi_ready, g + 1)
                nc.vector.tensor_tensor(yT_lo[:, b, :, :], yT[:, t, :, :], yT_hi[:, b, :, :].bitcast(F32),
                                        ALU.subtract).then_inc(yT_split, 1)

            def maximum(l, t, b, c):
                dve.wait_ge(scores_ready, C * (l * T + t) + c + 1)
                nc.vector.tensor_reduce(bank_max[:, b, c:c + 1], scores[:, c, :], AX_X,
                                        ALU.max).then_inc(bank_max_ready, 1)

            def negate_max(l, t, b):
                dve.wait_ge(bank_max_ready, C * (l * T + t + 1))
                nc.vector.tensor_reduce(neg_max[:, b:b + 1], bank_max[:, b, :], AX_X, ALU.max,
                                        negate=True).then_inc(neg_max_ready, 1)

            def mask(l, t, b):
                g = l * T + t
                dve.wait_ge(adj_loaded[b], 8 * (g - b) + 16)
                for c in range(C):
                    cols = slice(c * BANK, (c + 1) * BANK)
                    dve.wait_ge(probs_ready, C * g + c + 1)
                    nc.vector.tensor_tensor(probs[:, b, cols], probs[:, b, cols], adj_sb[:, b, cols],
                                            ALU.mult).then_inc(masked, 1)
                nc.vector.tensor_reduce(row_sum[:, b:b + 1], bank_sum[:, b, :], AX_X,
                                        ALU.add).then_inc(row_sum_ready, 1)
                dve.wait_ge(row_sum_ready, g + 1)
                nc.vector.reciprocal(inv_sum[:, b:b + 1], row_sum[:, b:b + 1]).then_inc(inv_sum_ready, 1)

            def probsT_rest(l, t, q):
                dve.wait_ge(probsT_hi_ready, Q * (l * T + t) + q + 1)
                nc.vector.tensor_tensor(probsT_lo[:, q, :], tp[:, BANK_OF_GROUP[q], :],
                                        probsT_hi[:, q, :].bitcast(F32), ALU.subtract
                                        ).then_inc(probsT_split, 1)

            def epilogue(l, t, b, reuse):
                g = l * T + t
                dve.wait_ge(pv_res_ready, g + 1)
                nc.vector.scalar_tensor_tensor(out=pv_sum[:, b, :], in0=pv_bank(t)[:, 0:D], scalar=inv_sum[:, b:b + 1],
                                               in1=pv_res[:, b, :], op0=ALU.mult, op1=ALU.add
                                               ).then_inc(pv_sum_ready, 1)
                dve.wait_ge(pv_sum_ready, g + 1)
                if l < L - 1:
                    dst = x_all[:, l + 1, t, :]
                else:
                    dst = x_last[:, b, :]
                    if reuse:
                        dve.wait_ge(resid_ready, t - 1)
                nc.vector.scalar_tensor_tensor(out=dst, in0=pv_sum[:, b, :], scalar=NEG_SLOPE,
                                               in1=pv_sum[:, b, :], op0=ALU.mult, op1=ALU.max
                                               ).then_inc(x_next_ready, 1)

            def statistics(t, b):
                dve.wait_ge(resid_ready, t + 1)
                nc.vector.bn_stats(stats[:, b, :], resid[:, b, :]).then_inc(stats_ready, 1)

            def aggregate(b):
                nc.vector.bn_aggr(mean_var[:, b, :], stats[:, b, :]).then_inc(mean_var_ready, 1)

            def normalise(t, b, reuse):
                if reuse:
                    dve.wait_ge(out_stored[b], 8 * (t - b))
                dve.wait_ge(inv_std_ready, t + 1)
                nc.vector.tensor_scalar(normed[:, b, :], resid[:, b, :], mean_var[:, b, 0:1],
                                        inv_std[:, b:b + 1], ALU.subtract, ALU.mult).then_inc(normed_ready, 1)

            def step(l, s, b, scoring=True, finish=True, split=True):
                first = isinstance(s, int)
                mask(l, s - 1, 1 - b)
                if split:
                    split_y(l, s + 1, 1 - b, True)
                if not scoring:
                    probsT_rest(l, s - 1, 0)
                    probsT_rest(l, s - 1, 1)
                if finish:
                    epilogue(l, s - 2, b, not (first and s < 4))
                if scoring:
                    for c in range(C - 1):
                        maximum(l, s, b, c)
                    probsT_rest(l, s - 1, 0)
                    probsT_rest(l, s - 1, 1)
                    maximum(l, s, b, C - 1)
                    negate_max(l, s, b)
                if l == L - 1 and not (first and s < 3):
                    normalise(s - 3, 1 - b, not (first and s < 5))
                if l == L - 1 and finish:
                    statistics(s - 2, b)
                    dve.wait_ge(stats_ready, s - 1)
                    probsT_rest(l, s - 1, 2)
                    aggregate(b)
                else:
                    probsT_rest(l, s - 1, 2)
                probsT_rest(l, s - 1, 3)

            def keys_step(l, t, b, stage=True):
                if stage:
                    stage_x(l, t + 3, 1 - b, True)
                xT_rest(l, t + 2, b, True)
                wh_rest(l, t, b)

            for l in range(L):
                if l == 0:
                    dve.wait_ge(x_loaded[0], 16)
                    stage_x(l, 0, 0, False)
                    stage_x(l, 1, 1, False)
                    split_wa(l)
                    xT_rest(l, 0, 0, False)
                    xT_rest(l, 1, 1, False)
                    dve.wait_ge(x_loaded[1], 16)
                stage_x(l, 2, 0, True)
                if l == 0:
                    wT_rest(l, 0)
                    wT_rest(l, 1)
                keys_step(l, 0, 0)
                keys_step(l, 1, 1)
                if l == 0:
                    dve.wait_ge(x_loaded[2], 16)
                with dve.Fori(1, T // 2 - 2) as u:
                    for b in range(2):
                        keys_step(l, 2 * u + b, b)
                if l == 0:
                    for later in range(1, L):
                        split_wa(later)
                        wT_rest(later, 0)
                        wT_rest(later, 1)
                keys_step(l, T - 4, 0)
                if l == 0:
                    m_rest(0)
                keys_step(l, T - 3, 1, stage=False)
                if l == 0:
                    for later in range(1, L):
                        m_rest(later)
                wh_rest(l, T - 2, 0)
                wh_rest(l, T - 1, 1)

                store_y(l, 0)
                split_y(l, 0, 0, l > 0)
                split_y(l, 1, 1, l > 0)
                for c in range(C):
                    maximum(l, 0, 0, c)
                negate_max(l, 0, 0)
                for n in range(1, C):
                    store_y(l, n)

                step(l, 1, 1, finish=False)
                for t in range(2, 6):
                    step(l, t, t % 2)
                with dve.Fori(3, T // 2 - 1) as u:
                    for b in range(2):
                        step(l, 2 * u + b, b)
                step(l, T - 2, 0)
                step(l, T - 1, 1, split=False)
                step(l, T, 0, scoring=False, split=False)
                if l < L - 1:
                    stage_x(l + 1, 0, 0, True)
                    stage_x(l + 1, 1, 1, True)
                    xT_rest(l + 1, 0, 0, True)
                    xT_rest(l + 1, 1, 1, True)
                    epilogue(l, T - 1, 1, True)
                else:
                    normalise(T - 2, 0, True)
                    epilogue(l, T - 1, 1, True)
                    statistics(T - 1, 1)
                    dve.wait_ge(stats_ready, T)
                    aggregate(1)
                    normalise(T - 1, 1, True)

        @block.tensor
        def _(pe):
            def transpose_x(l, t, b, reuse):
                g = l * T + t
                pe.wait_ge(x_staged, g + 1)
                if reuse:
                    pe.wait_ge(xT_split, g - 1)
                for k in range(K):
                    mm = nc.tensor.transpose(tp[:, b, k * P:(k + 1) * P], x_stage[:, b, k * P:(k + 1) * P],
                                             ident[:])
                mm.then_inc(xT_ready, 1)

            def transpose_w(l):
                pe.wait_ge(w_loaded[l], 16)
                for h in range(2):
                    for m in range(K):
                        for k in range(K):
                            mm = nc.tensor.transpose(wT_bank[l][h][:, m * D + k * P:m * D + (k + 1) * P],
                                                     w_raw[:, l, k, h * D + m * P:h * D + (m + 1) * P], ident[:])
                    mm.then_inc(wT_ready, 1)

            def make_m(l):
                pe.wait_ge(wT_split, 2 * l + 2)
                (a_hi, a_lo), (b_hi, b_lo) = wT(l, 0), wT(l, 1)
                for k in range(K):
                    rows, dst = slice(k * P, (k + 1) * P), m_bank[l][:, k * D:(k + 1) * D]
                    for m in range(K):
                        nc.tensor.matmul(dst, a_hi[:, m, rows], b_hi[:, m, :], start=(m == 0), stop=False)
                        nc.tensor.matmul(dst, a_hi[:, m, rows], b_lo[:, m, :], start=False, stop=False)
                        mm = nc.tensor.matmul(dst, a_lo[:, m, rows], b_hi[:, m, :], start=False,
                                              stop=(m == K - 1))
                mm.then_inc(m_ready, 1)

            def project(l, t, b, reuse):
                g = l * T + t
                pe.wait_ge(xT_split, g + 1)
                if reuse:
                    pe.wait_ge(wh_split, g - 1)
                for k in range(K):
                    nc.tensor.matmul(wh_bank[b], xT_hi[:, b, k, :], wa_hi[:, l, k, :], start=(k == 0), stop=False)
                    nc.tensor.matmul(wh_bank[b], xT_hi[:, b, k, :], wa_lo[:, l, k, :], start=False, stop=False)
                    mm = nc.tensor.matmul(wh_bank[b], xT_lo[:, b, k, :], wa_hi[:, l, k, :],
                                          start=False, stop=(k == K - 1))
                mm.then_inc(wh_ready, 1)

            def queries(l, n):
                if n >= 2:
                    pe.wait_ge(y_stored, K * (l * C + n - 1))
                cols = slice(n * BANK, (n + 1) * BANK)
                for f in range(K):
                    dst, rows = y_bank[n % 2][f], slice(f * P, (f + 1) * P)
                    for k in range(K):
                        nc.tensor.matmul(dst, m_hi[:, l, k, rows], keys_hi[:, k, cols], start=(k == 0), stop=False)
                        nc.tensor.matmul(dst, m_hi[:, l, k, rows], keys_lo[:, k, cols], start=False, stop=False)
                        mm = nc.tensor.matmul(dst, m_lo[:, l, k, rows], keys_hi[:, k, cols],
                                              start=False, stop=(k == K - 1))
                    mm.then_inc(y_ready, 1)

            def score(l, t, b, c):
                for k in range(K):
                    cols = slice(c * BANK, (c + 1) * BANK)
                    nc.tensor.matmul(scores[:, c, :], yT_hi[:, b, k, :], keys_hi[:, k, cols],
                                     start=(k == 0), stop=False)
                    nc.tensor.matmul(scores[:, c, :], yT_hi[:, b, k, :], keys_lo[:, k, cols],
                                     start=False, stop=False)
                    mm = nc.tensor.matmul(scores[:, c, :], yT_lo[:, b, k, :], keys_hi[:, k, cols],
                                          start=False, stop=(k == K - 1))
                mm.then_inc(scores_ready, 1)

            def transpose_probs(l, t, b, q):
                g = l * T + t
                pe.wait_ge(masked, C * g + q + 1)
                bank = BANK_OF_GROUP[q]
                if q >= TP_BANKS:
                    pe.wait_ge(probsT_split, Q * g + q - TP_BANKS + 1)
                elif not (isinstance(t, int) and g == 0):
                    held = max(r for r in range(Q) if BANK_OF_GROUP[r] == bank)
                    pe.wait_ge(probsT_split, Q * (g - 1) + held + 1)
                for j in range(JB):
                    lhs = probs[:, b, (q * JB + j) * P:(q * JB + j + 1) * P]
                    mm = nc.tensor.transpose(tp[:, bank, j * P:(j + 1) * P], lhs, ident[:])
                mm.then_inc(probsT_ready, 1)

            def weigh(l, t, q):
                g = l * T + t
                pe.wait_ge(probsT_split, Q * g + q + 1)
                bank = pv_bank(t)
                if q == 0 and not (isinstance(t, int) and t in (0, T - 1)):
                    pe.wait_ge(pv_sum_ready, g)
                for j in range(JB):
                    first, final = q == 0 and j == 0, q == Q - 1 and j == JB - 1
                    rows = q * JB + j
                    hi, lo = (a[:, q, j * P:(j + 1) * P] for a in (probsT_hi, probsT_lo))

                    def with_lo():
                        nc.tensor.matmul(bank[:, 0:D], lo, wh[:, rows, 0:D], start=False, stop=False)

                    if final:
                        with_lo()
                    mm = nc.tensor.matmul(bank, hi, wh[:, rows, :], start=first, stop=final)
                    if not final:
                        with_lo()
                if q == Q - 1:
                    mm.then_inc(pv_ready, 1)

            def step(l, s, b):
                g = l * T + s
                pe.wait_ge(yT_split, g + 1)
                for c in range(C):
                    if c == C - 1:
                        transpose_probs(l, s - 1, 1 - b, 0)
                        transpose_probs(l, s - 1, 1 - b, 1)
                    pe.wait_ge(probs_ready, C * (g - 1) + c + 1)
                    score(l, s, b, c)
                value_rest(l, s - 1, 1 - b, s)

            def value_rest(l, t, b, s):
                transpose_probs(l, t, b, 2)
                weigh(l, t, 0)
                transpose_probs(l, t, b, 3)
                weigh(l, t, 1)
                weigh(l, t, 2)
                if isinstance(s, int) and s == T - 1:
                    transpose_probs(l, T - 1, 1, 0)
                    transpose_probs(l, T - 1, 1, 1)
                if isinstance(s, int) and s == T and l < L - 1:
                    transpose_x(l + 1, 0, 0, True)
                    transpose_x(l + 1, 1, 1, True)
                weigh(l, t, 3)

            def keys_step(l, t, b, reuse=True):
                transpose_x(l, t + 2, b, True)
                project(l, t, b, reuse)

            pe.wait_ge(consts_ready, 2)
            transpose_x(0, 0, 0, False)
            transpose_x(0, 1, 1, False)
            transpose_w(0)
            pe.wait_ge(wa_split, 1)
            for l in range(L):
                keys_step(l, 0, 0, l > 0)
                keys_step(l, 1, 1, l > 0)
                with pe.Fori(1, T // 2 - 2) as u:
                    for b in range(2):
                        keys_step(l, 2 * u + b, b)
                if l == 0:
                    for later in range(1, L):
                        transpose_w(later)
                keys_step(l, T - 4, 0)
                if l == 0:
                    make_m(0)
                keys_step(l, T - 3, 1)
                if l == 0:
                    for later in range(1, L):
                        make_m(later)
                project(l, T - 2, 0, True)
                project(l, T - 1, 1, True)

                pe.wait_ge(m_split, L)
                pe.wait_ge(wa_split, L)
                pe.wait_ge(keys_hi_ready, (l + 1) * T)
                pe.wait_ge(keys_lo_ready, (l + 1) * T)
                queries(l, 0)
                queries(l, 1)
                pe.wait_ge(yT_split, l * T + 1)
                for c in range(C):
                    if c == 2:
                        pe.wait_ge(wh_split, (l + 1) * T)
                    score(l, 0, 0, c)
                for n in range(2, C):
                    queries(l, n)

                step(l, 1, 1)
                with pe.Fori(1, T // 2 - 1) as u:
                    for b in range(2):
                        step(l, 2 * u + b, b)
                step(l, T - 2, 0)
                step(l, T - 1, 1)
                value_rest(l, T - 1, 1, T)


_INS = ['x', 'adj', 'L0_gnn_W_stack']
_OUTS = [((2048, 256), 'float32')]


def kernel(**inputs):
    import numpy as _np
    import concourse.bacc as _bacc
    from concourse import mybir as _mybir
    from concourse.bass_utils import run_bass_kernel_spmd as _run

    nc = _bacc.Bacc("TRN2", target_bir_lowering=False, num_devices=1)
    arrays, args = {}, []
    for name in _INS:
        a = _np.ascontiguousarray(inputs[name])
        arrays[f"in_{name}_dram"] = a
        args.append(nc.dram_tensor(f"in_{name}_dram", a.shape, _mybir.dt.from_np(a.dtype), kind="ExternalInput").ap())
    for i, (shape, dtype) in enumerate(_OUTS):
        dt = _mybir.dt.from_np(_np.dtype(dtype))
        args.append(nc.dram_tensor(f"out_{i}_dram", shape, dt, kind="ExternalOutput").ap())
    gat_resnorm_kernel(nc, *args)
    r = _run(nc, [arrays], core_ids=[0])
    got = tuple(r.results[0][f"out_{i}_dram"] for i in range(len(_OUTS)))
    return got[0]
```

```python
from contextlib import ExitStack

import concourse.bass as bass
from concourse import mybir

F32 = mybir.dt.float32
F32R = mybir.dt.float32r
ALU = mybir.AluOpType
ACT = mybir.ActivationFunctionType
AX_X = mybir.AxisListType.X

P = 128
BANK = 512
NEG_SLOPE = 0.01
EPS = 1e-05


def gat_resnorm_kernel(nc: bass.Bass, x: bass.AP, adj: bass.AP, W: bass.AP, out: bass.AP):
    N, D = x.shape
    L = W.shape[0]
    T = N // P
    K = D // P
    C = N // BANK
    Q = C
    JB = BANK // P
    TPG = T // C
    X_PARTS = [(0, 1), (1, 2), (2, 5), (5, T)]
    TP_BANKS = 3
    BANK_OF_GROUP = [q % TP_BANKS for q in range(Q)]
    WARM_UP = 12
    XB = 4
    assert L == 2 and K == 2 and C == 4 and T % 2 == 0 and T >= 8 and 2 * D == BANK

    x_dram = x.rearrange("(t p) d -> p t d", p=P)
    adj_dram = adj.rearrange("(t p) n -> t p n", p=P)
    out_dram = out.rearrange("(t p) d -> t p d", p=P)
    w_dram = W.rearrange("l (k p) c -> l p k c", p=P)

    with ExitStack() as ctx:
        def sb(name, shape, dt=F32):
            return ctx.enter_context(nc.sbuf_tensor(name, shape, dt))

        def sem(name):
            return ctx.enter_context(nc.semaphore(name))

        scores = ctx.enter_context(nc.psum_tensor("scores", [P, C, BANK], F32))
        tp = ctx.enter_context(nc.psum_tensor("tp", [P, TP_BANKS, BANK], F32))
        pv = ctx.enter_context(nc.psum_tensor("pv", [P, BANK], F32))

        ident = sb("ident", [P, P])
        w_raw = sb("w_raw", [P, L, K, 2 * D])
        wa_hi = sb("wa_hi", [P, L, K, D], F32R)
        wa_lo = sb("wa_lo", [P, L, K, D], F32R)
        m_hi = sb("m_hi", [P, L, K, D], F32R)
        m_lo = sb("m_lo", [P, L, K, D], F32R)
        x_all = sb("x_all", [P, L, T, D])
        x_stage = sb("x_stage", [P, 2, D])
        keys_hi = sb("keys_hi", [P, K, N], F32R)
        keys_lo = sb("keys_lo", [P, K, N], F32R)
        wh = sb("wh", [P, T, 2 * D], F32R)
        yT = sb("yT", [P, T, K, P])
        yT_hi = sb("yT_hi", [P, 2, K, P], F32R)
        yT_lo = sb("yT_lo", [P, 2, K, P], F32R)
        adj_sb = sb("adj_sb", [P, 2, N])
        probs = sb("probs", [P, 2, N])
        probsT_hi = sb("probsT_hi", [P, Q, BANK], F32R)
        probsT_lo = sb("probsT_lo", [P, Q, BANK], F32R)
        bank_max = sb("bank_max", [P, 2, C])
        neg_max = sb("neg_max", [P, 2])
        bank_sum = sb("bank_sum", [P, 2, C])
        row_sum = sb("row_sum", [P, 2])
        inv_sum = sb("inv_sum", [P, 2])
        pv_lo = sb("pv_lo", [P, 2, D])
        pv_res = sb("pv_res", [P, 2, D])
        pv_sum = sb("pv_sum", [P, 2, D])
        x_last = sb("x_last", [P, 2, D])
        resid = sb("resid", [P, 2, D])
        stats = sb("stats", [P, 2, nc.vector.BN_STATS_DIM])
        mean_var = sb("mean_var", [P, 2, 2])
        var_eps = sb("var_eps", [P, 2])
        inv_std = sb("inv_std", [P, 2])
        minus_half = sb("minus_half", [P, 1])
        eps = sb("eps", [P, 1])
        normed = sb("normed", [P, 2, D])

        w_loaded = [sem(f"w_loaded{l}") for l in range(L)]
        x_loaded = [sem(f"x_loaded{i}") for i in range(len(X_PARTS))]
        adj_loaded = [sem("adj_loaded0"), sem("adj_loaded1")]
        out_stored = [sem("out_stored0"), sem("out_stored1")]
        consts_ready = sem("consts_ready")
        wa_hi_ready = sem("wa_hi_ready")
        wa_split = sem("wa_split")
        wT_ready = sem("wT_ready")
        wT_hi_ready = sem("wT_hi_ready")
        wT_split = sem("wT_split")
        m_ready = sem("m_ready")
        m_hi_ready = sem("m_hi_ready")
        m_split = sem("m_split")
        x_staged = sem("x_staged")
        xT_ready = sem("xT_ready")
        xT_hi_ready = sem("xT_hi_ready")
        xT_split = sem("xT_split")
        keys_hi_ready = sem("keys_hi_ready")
        keys_lo_ready = sem("keys_lo_ready")
        wh_ready = sem("wh_ready")
        wh_hi_ready = sem("wh_hi_ready")
        wh_split = sem("wh_split")
        y_ready = sem("y_ready")
        y_stored = sem("y_stored")
        yT_hi_ready = sem("yT_hi_ready")
        yT_split = sem("yT_split")
        scores_ready = sem("scores_ready")
        bank_max_ready = sem("bank_max_ready")
        neg_max_ready = sem("neg_max_ready")
        probs_ready = sem("probs_ready")
        row_sum_ready = sem("row_sum_ready")
        inv_sum_ready = sem("inv_sum_ready")
        masked = sem("masked")
        probsT_ready = sem("probsT_ready")
        probsT_hi_ready = sem("probsT_hi_ready")
        probsT_split = sem("probsT_split")
        pv_ready = sem("pv_ready")
        pv_lo_ready = sem("pv_lo_ready")
        pv_res_ready = sem("pv_res_ready")
        pv_sum_ready = sem("pv_sum_ready")
        x_next_ready = sem("x_next_ready")
        resid_ready = sem("resid_ready")
        stats_ready = sem("stats_ready")
        mean_var_ready = sem("mean_var_ready")
        var_eps_ready = sem("var_eps_ready")
        inv_std_ready = sem("inv_std_ready")
        last_resid_ready = sem("last_resid_ready")
        normed_ready = sem("normed_ready")

        xT_hi, xT_lo = (a[:, 0:Q // 2, :].rearrange("p q (t k i) -> p (q t) k i", k=K, i=P)
                        for a in (probsT_hi, probsT_lo))

        def wT(h):
            return (a[:, Q // 2 + h, :].rearrange("p (m k) -> p m k", m=K) for a in (probsT_hi, probsT_lo))

        wT_bank = [tp[:, 2, :], pv[:, :]]
        m_bank = [pv[:, :], tp[:, 0, :]]
        y_bank = [[tp[:, 0, :], tp[:, 1, :]], [tp[:, 2, :], pv[:, :]]]
        wh_bank = [scores[:, (i + 1) % XB, 0:D] for i in range(XB)]

        def pv_bank(t):
            return scores[:, 0, :] if isinstance(t, int) and t == T - 1 else pv[:, :]

        def by_k(bank):
            return bank.rearrange("p (k i) -> p k i", k=K)

        block = ctx.enter_context(nc.Block())

        @block.sync
        def _(sp):
            def load_adj(t, b):
                sp.dma_start(adj_sb[:, b, :], adj_dram[t]).then_inc(adj_loaded[b], 16)

            def store_out(t, b):
                sp.wait_ge(normed_ready, t + 1)
                sp.dma_start(out_dram[t], normed[:, b, :]).then_inc(out_stored[b], 16)

            def load_x(i):
                part = slice(*X_PARTS[i])
                sp.dma_start(x_all[:, 0, part, :], x_dram[:, part, :]).then_inc(x_loaded[i], 16)

            def load_w(l):
                sp.dma_start(w_raw[:, l, :, :], w_dram[l]).then_inc(w_loaded[l], 16)

            load_x(0)
            load_x(1)
            load_w(0)
            load_x(2)
            load_x(3)
            for l in range(1, L):
                load_w(l)
            load_adj(0, 0)
            load_adj(1, 1)
            with sp.Fori(1, T // 2) as u:
                for b in range(2):
                    sp.wait_ge(masked, C * (2 * u + b - 1))
                    load_adj(2 * u + b, b)
            for b in range(2):
                sp.wait_ge(masked, C * (T + b - 1))
                load_adj(b, b)
            for b in range(2):
                sp.wait_ge(masked, C * (T + b + 1))
                load_adj(2 + b, b)
            with sp.Fori(2, T // 2) as u:
                for b in range(2):
                    sp.wait_ge(masked, C * (T + 2 * u + b - 1))
                    load_adj(2 * u + b, b)
                    store_out(2 * u + b - 4, b)
            for t in range(T - 4, T):
                store_out(t, t % 2)
            for b in range(2):
                sp.wait_ge(out_stored[b], 16 * (T // 2))

        @block.gpsimd
        def _(pool):
            nc.gpsimd.memset(ident[:], 0.0).then_inc(consts_ready, 1)
            pool.wait_ge(consts_ready, 1)
            nc.gpsimd.affine_select(out=ident[:], in_=ident[:], compare_op=ALU.not_equal, fill=1.0,
                                    base=0, pattern=[[-1, P]], channel_multiplier=1).then_inc(consts_ready, 1)
            nc.gpsimd.memset(minus_half[:], -0.5).then_inc(consts_ready, 1)
            nc.gpsimd.memset(eps[:], EPS).then_inc(consts_ready, 1)
            pool.wait_ge(consts_ready, 4)

            def copy_keys_lo(l, t, i):
                g = l * T + t
                pool.wait_ge(xT_split, g + 1)
                nc.gpsimd.tensor_copy(keys_lo[:, :, bass.ts(t, P)], xT_lo[:, i, :, :].bitcast(F32)
                                      ).then_inc(keys_lo_ready, 1)

            def add_x(l, t, b):
                pool.wait_ge(pv_lo_ready, l * (T - 1) + t + 1)
                nc.gpsimd.tensor_tensor(pv_res[:, b, :], pv_lo[:, b, :], x_all[:, l, t, :],
                                        ALU.add).then_inc(pv_res_ready, 1)

            def add_resid(t, b, reuse):
                pool.wait_ge(x_next_ready, T * (L - 1) + t + 1)
                if reuse:
                    pool.wait_ge(normed_ready, t - 1)
                nc.gpsimd.tensor_tensor(resid[:, b, :], x_last[:, b, :], x_all[:, 0, t, :],
                                        ALU.add).then_inc(resid_ready, 1)

            def inverse_std(t, b):
                pool.wait_ge(mean_var_ready, t + 1)
                nc.gpsimd.tensor_tensor(var_eps[:, b:b + 1], mean_var[:, b, 1:2], eps[:],
                                        ALU.add).then_inc(var_eps_ready, 1)
                pool.wait_ge(var_eps_ready, t + 1)
                nc.gpsimd.tensor_tensor(inv_std[:, b:b + 1], var_eps[:, b:b + 1], minus_half[:],
                                        ALU.pow).then_inc(inv_std_ready, 1)

            for l in range(L):
                last = l == L - 1
                if l == 0:
                    copy_keys_lo(l, 0, 0)
                for t in range(1, XB):
                    copy_keys_lo(l, t, t)
                with pool.Fori(1, T // XB) as u:
                    for i in range(XB):
                        copy_keys_lo(l, XB * u + i, i)
                if not last:
                    with pool.Fori(0, T // 2 - 1) as u:
                        for b in range(2):
                            add_x(l, 2 * u + b, b)
                    add_x(l, T - 2, 0)
                    copy_keys_lo(l + 1, 0, 0)
                else:
                    for t in range(4):
                        add_x(l, t, t % 2)
                        if t:
                            inverse_std(t - 1, 1 - t % 2)
                        add_resid(t, t % 2, t >= 2)
                    with pool.Fori(2, T // 2 - 1) as u:
                        for b in range(2):
                            add_x(l, 2 * u + b, b)
                            inverse_std(2 * u + b - 1, 1 - b)
                            add_resid(2 * u + b, b, True)
                    add_x(l, T - 2, 0)
                    inverse_std(T - 3, 1)
                    add_resid(T - 2, 0, True)
                    inverse_std(T - 2, 0)
                    inverse_std(T - 1, 1)

        @block.scalar
        def _(act):
            def wT_round(l, h):
                act.wait_ge(wT_ready, 2 * l + h + 1)
                hi, _ = wT(h)
                nc.scalar.copy(hi, by_k(wT_bank[h])).then_inc(wT_hi_ready, 1)

            def m_round(l):
                act.wait_ge(m_ready, l + 1)
                nc.scalar.copy(m_hi[:, l, :, :], by_k(m_bank[l])).then_inc(m_hi_ready, 1)

            def xT_round(l, t, i, reuse):
                g = l * T + t
                act.wait_ge(xT_ready, g + 1)
                if reuse:
                    act.wait_ge(keys_hi_ready, g - XB + 1)
                    act.wait_ge(wh_ready, g - XB + 1)
                nc.scalar.copy(xT_hi[:, i, :, :], by_k(tp[:, i % 2, 0:D])).then_inc(xT_hi_ready, 1)

            def copy_keys_hi(l, t, i):
                act.wait_ge(xT_hi_ready, l * T + t + 1)
                nc.scalar.copy(keys_hi[:, :, bass.ts(t, P)], xT_hi[:, i, :, :].bitcast(F32)
                               ).then_inc(keys_hi_ready, 1)

            def wh_round(l, t, i):
                act.wait_ge(wh_ready, l * T + t + 1)
                nc.scalar.copy(wh[:, t, 0:D], wh_bank[i]).then_inc(wh_hi_ready, 1)

            def scale_pv_lo(l, t, b):
                g = l * T + t
                act.wait_ge(pv_ready, g + 1)
                act.wait_ge(inv_sum_ready, g + 1)
                nc.scalar.activation(pv_lo[:, b, :], pv[:, D:2 * D], ACT.Copy,
                                     scale=inv_sum[:, b:b + 1]).then_inc(pv_lo_ready, 1)

            def probsT_round(l, t, q):
                act.wait_ge(probsT_ready, Q * (l * T + t) + q + 1)
                nc.scalar.copy(probsT_hi[:, q, :], tp[:, BANK_OF_GROUP[q], :]).then_inc(probsT_hi_ready, 1)

            def exponentials(l, t, b):
                g = l * T + t
                act.wait_ge(neg_max_ready, g + 1)
                for c in range(C):
                    nc.scalar.activation(probs[:, b, c * BANK:(c + 1) * BANK], scores[:, c, :], ACT.Exp,
                                         bias=neg_max[:, b:b + 1], accum_out=bank_sum[:, b, c:c + 1]
                                         ).then_inc(probs_ready, 1)

            def first_rounds(l):
                xT_round(l, 0, 0, l > 0)
                xT_round(l, 1, 1, l > 0)

            def keys_step(l, t, i):
                xT_round(l, t + 2, (i + 2) % XB, l > 0 or not (isinstance(t, int) and t + 2 < XB))
                copy_keys_hi(l, t + 1, (i + 1) % XB)
                if not (isinstance(t, int) and t == 0):
                    wh_round(l, t - 1, (i - 1) % XB)

            first_rounds(0)
            wT_round(0, 0)
            wT_round(0, 1)
            for l in range(L):
                copy_keys_hi(l, 0, 0)
                for t in range(XB):
                    keys_step(l, t, t)
                if l == 0:
                    m_round(0)
                with act.Fori(1, T // XB - 1) as u:
                    for i in range(XB):
                        keys_step(l, XB * u + i, i)
                keys_step(l, T - 4, 0)
                keys_step(l, T - 3, 1)
                copy_keys_hi(l, T - 1, XB - 1)
                for t in range(T - 3, T):
                    wh_round(l, t, t % XB)
                if l == 0:
                    wT_round(1, 0)
                    wT_round(1, 1)

                exponentials(l, 0, 0)
                if l == 0:
                    m_round(1)
                for q in range(Q):
                    probsT_round(l, 0, q)
                exponentials(l, 1, 1)
                with act.Fori(1, T // 2) as u:
                    for b in range(2):
                        s = 2 * u + b
                        scale_pv_lo(l, s - 2, b)
                        for q in range(Q):
                            probsT_round(l, s - 1, q)
                        exponentials(l, s, b)
                probsT_round(l, T - 1, 0)
                probsT_round(l, T - 1, 1)
                scale_pv_lo(l, T - 2, 0)
                probsT_round(l, T - 1, 2)
                probsT_round(l, T - 1, 3)
                if l < L - 1:
                    first_rounds(l + 1)

        @block.vector
        def _(dve):
            def split_wa(l):
                dve.wait_ge(w_loaded[l], 16)
                nc.vector.tensor_copy(wa_hi[:, l, :, :], w_raw[:, l, :, 0:D]).then_inc(wa_hi_ready, 1)
                dve.wait_ge(wa_hi_ready, l + 1)
                nc.vector.tensor_tensor(wa_lo[:, l, :, :], w_raw[:, l, :, 0:D], wa_hi[:, l, :, :].bitcast(F32),
                                        ALU.subtract).then_inc(wa_split, 1)

            def wT_rest(l, h):
                dve.wait_ge(wT_hi_ready, 2 * l + h + 1)
                hi, lo = wT(h)
                nc.vector.tensor_tensor(lo, by_k(wT_bank[h]), hi.bitcast(F32),
                                        ALU.subtract).then_inc(wT_split, 1)

            def m_rest(l):
                dve.wait_ge(m_hi_ready, l + 1)
                nc.vector.tensor_tensor(m_lo[:, l, :, :], by_k(m_bank[l]), m_hi[:, l, :, :].bitcast(F32),
                                        ALU.subtract).then_inc(m_split, 1)

            def stage_x(l, t, b, reuse):
                if reuse:
                    dve.wait_ge(xT_ready, l * T + t - 1)
                if l > 0:
                    dve.wait_ge(x_next_ready, (l - 1) * T + t + 1)
                nc.vector.tensor_copy(x_stage[:, b, :], x_all[:, l, t, :]).then_inc(x_staged, 1)

            def xT_rest(l, t, i, reuse):
                g = l * T + t
                if reuse:
                    dve.wait_ge(keys_lo_ready, g - XB + 1)
                dve.wait_ge(xT_hi_ready, g + 1)
                nc.vector.tensor_tensor(xT_lo[:, i, :, :], by_k(tp[:, i % 2, 0:D]),
                                        xT_hi[:, i, :, :].bitcast(F32), ALU.subtract).then_inc(xT_split, 1)

            def wh_rest(l, t, i):
                dve.wait_ge(wh_hi_ready, l * T + t + 1)
                nc.vector.tensor_tensor(wh[:, t, D:2 * D], wh_bank[i], wh[:, t, 0:D].bitcast(F32),
                                        ALU.subtract).then_inc(wh_split, 1)

            def store_y(l, n):
                for k in range(K):
                    dve.wait_ge(y_ready, K * (l * C + n) + k + 1)
                    nc.vector.tensor_copy(yT[:, n * TPG:(n + 1) * TPG, k, :],
                                          y_bank[n % 2][k].rearrange("p (t i) -> p t i", t=TPG)
                                          ).then_inc(y_stored, 1)

            def split_y(l, t, b, reuse):
                g = l * T + t
                if reuse:
                    dve.wait_ge(scores_ready, C * (g - 1))
                if isinstance(t, int) and t == 0:
                    dve.wait_ge(y_stored, K * (l * C + 1))
                if isinstance(t, int) and t == TPG:
                    dve.wait_ge(y_stored, K * (l + 1) * C)
                nc.vector.tensor_copy(yT_hi[:, b, :, :], yT[:, t, :, :]).then_inc(yT_hi_ready, 1)
                dve.wait_ge(yT_hi_ready, g + 1)
                nc.vector.tensor_tensor(yT_lo[:, b, :, :], yT[:, t, :, :], yT_hi[:, b, :, :].bitcast(F32),
                                        ALU.subtract).then_inc(yT_split, 1)

            def maximum(l, t, b, c):
                dve.wait_ge(scores_ready, C * (l * T + t) + c + 1)
                nc.vector.tensor_reduce(bank_max[:, b, c:c + 1], scores[:, c, :], AX_X,
                                        ALU.max).then_inc(bank_max_ready, 1)

            def negate_max(l, t, b):
                dve.wait_ge(bank_max_ready, C * (l * T + t + 1))
                nc.vector.tensor_reduce(neg_max[:, b:b + 1], bank_max[:, b, :], AX_X, ALU.max,
                                        negate=True).then_inc(neg_max_ready, 1)

            def mask(l, t, b):
                g = l * T + t
                dve.wait_ge(adj_loaded[b], 8 * (g - b) + 16)
                for c in range(C):
                    cols = slice(c * BANK, (c + 1) * BANK)
                    dve.wait_ge(probs_ready, C * g + c + 1)
                    nc.vector.tensor_tensor(probs[:, b, cols], probs[:, b, cols], adj_sb[:, b, cols],
                                            ALU.mult).then_inc(masked, 1)
                nc.vector.tensor_reduce(row_sum[:, b:b + 1], bank_sum[:, b, :], AX_X,
                                        ALU.add).then_inc(row_sum_ready, 1)
                dve.wait_ge(row_sum_ready, g + 1)
                nc.vector.reciprocal(inv_sum[:, b:b + 1], row_sum[:, b:b + 1]).then_inc(inv_sum_ready, 1)

            def probsT_rest(l, t, q):
                dve.wait_ge(probsT_hi_ready, Q * (l * T + t) + q + 1)
                nc.vector.tensor_tensor(probsT_lo[:, q, :], tp[:, BANK_OF_GROUP[q], :],
                                        probsT_hi[:, q, :].bitcast(F32), ALU.subtract
                                        ).then_inc(probsT_split, 1)

            def add_values(l, t, b):
                if isinstance(t, int) and t == T - 1:
                    dve.wait_ge(pv_ready, l * T + t + 1)
                    dve.wait_ge(inv_sum_ready, l * T + t + 1)
                    rest = x_all[:, l, t, :]
                else:
                    dve.wait_ge(pv_res_ready, l * (T - 1) + t + 1)
                    rest = pv_res[:, b, :]
                nc.vector.scalar_tensor_tensor(out=pv_sum[:, b, :], in0=pv_bank(t)[:, 0:D],
                                               scalar=inv_sum[:, b:b + 1], in1=rest,
                                               op0=ALU.mult, op1=ALU.add).then_inc(pv_sum_ready, 1)

            def leaky_relu(l, t, b, reuse):
                g = l * T + t
                dve.wait_ge(pv_sum_ready, g + 1)
                if l < L - 1:
                    dst = x_all[:, l + 1, t, :]
                else:
                    dst = x_last[:, b, :]
                    if reuse:
                        dve.wait_ge(resid_ready, t - 1)
                nc.vector.scalar_tensor_tensor(out=dst, in0=pv_sum[:, b, :], scalar=NEG_SLOPE,
                                               in1=pv_sum[:, b, :], op0=ALU.mult, op1=ALU.max
                                               ).then_inc(x_next_ready, 1)

            def statistics(t, b):
                dve.wait_ge(resid_ready, t + 1)
                nc.vector.bn_stats(stats[:, b, :], resid[:, b, :]).then_inc(stats_ready, 1)

            def aggregate(b):
                nc.vector.bn_aggr(mean_var[:, b, :], stats[:, b, :]).then_inc(mean_var_ready, 1)

            def normalise(t, b, reuse):
                if reuse:
                    dve.wait_ge(out_stored[b], 8 * (t - b))
                dve.wait_ge(inv_std_ready, t + 1)
                nc.vector.tensor_scalar(normed[:, b, :], resid[:, b, :], mean_var[:, b, 0:1],
                                        inv_std[:, b:b + 1], ALU.subtract, ALU.mult).then_inc(normed_ready, 1)

            def step(l, s, b, scoring=True, finish=True, split=True, masking=True):
                first = isinstance(s, int)
                if masking:
                    mask(l, s - 1, 1 - b)
                if split:
                    split_y(l, s + 1, 1 - b, True)
                if not scoring:
                    probsT_rest(l, s - 1, 0)
                    probsT_rest(l, s - 1, 1)
                    probsT_rest(l, s - 1, 2)
                    probsT_rest(l, s - 1, 3)
                if finish:
                    add_values(l, s - 2, b)
                    leaky_relu(l, s - 2, b, not (first and s < 4))
                if scoring:
                    for c in range(C - 1):
                        maximum(l, s, b, c)
                    probsT_rest(l, s - 1, 0)
                    probsT_rest(l, s - 1, 1)
                    maximum(l, s, b, C - 1)
                    negate_max(l, s, b)
                if l == L - 1 and not (first and s < 3):
                    normalise(s - 3, 1 - b, not (first and s < 5))
                if l == L - 1 and finish:
                    statistics(s - 2, b)
                    dve.wait_ge(stats_ready, s - 1)
                    if scoring:
                        probsT_rest(l, s - 1, 2)
                    aggregate(b)
                elif scoring:
                    probsT_rest(l, s - 1, 2)
                if scoring:
                    probsT_rest(l, s - 1, 3)

            def last_epilogue(l, b):
                t = T - 1
                add_values(l, t, b)
                leaky_relu(l, t, b, True)
                dve.wait_ge(x_next_ready, (l + 1) * T)
                nc.vector.tensor_tensor(resid[:, b, :], x_last[:, b, :], x_all[:, 0, t, :],
                                        ALU.add).then_inc(last_resid_ready, 1)
                dve.wait_ge(last_resid_ready, 1)
                nc.vector.bn_stats(stats[:, b, :], resid[:, b, :]).then_inc(stats_ready, 1)

            def keys_step(l, t, i, stage=True):
                if stage:
                    stage_x(l, t + 3, (i + 1) % 2, True)
                if not (isinstance(t, int) and t < 2):
                    wh_rest(l, t - 2, (i - 2) % XB)
                xT_rest(l, t + 2, (i + 2) % XB, l > 0 or not (isinstance(t, int) and t + 2 < XB))

            for l in range(L):
                if l == 0:
                    dve.wait_ge(x_loaded[0], 16)
                    stage_x(l, 0, 0, False)
                    dve.wait_ge(x_loaded[1], 16)
                    stage_x(l, 1, 1, False)
                    split_wa(l)
                    xT_rest(l, 0, 0, False)
                    xT_rest(l, 1, 1, False)
                    dve.wait_ge(x_loaded[2], 16)
                    stage_x(l, 2, 0, True)
                    wT_rest(l, 0)
                    wT_rest(l, 1)
                for t in range(XB):
                    if l == 0 and t + 3 == X_PARTS[3][0]:
                        dve.wait_ge(x_loaded[3], 16)
                    keys_step(l, t, t)
                    if l > 0 and t == 1:
                        add_values(l - 1, T - 1, 1)
                    if l > 0 and t == 2:
                        leaky_relu(l - 1, T - 1, 1, True)
                if l == 0:
                    m_rest(0)
                with dve.Fori(1, T // XB - 1) as u:
                    for i in range(XB):
                        keys_step(l, XB * u + i, i)
                keys_step(l, T - 4, 0)
                keys_step(l, T - 3, 1, stage=False)
                for t in range(T - 4, T):
                    wh_rest(l, t, t % XB)
                if l == 0:
                    wT_rest(1, 0)
                    wT_rest(1, 1)

                store_y(l, 0)
                split_y(l, 0, 0, l > 0)
                split_y(l, 1, 1, l > 0)
                for c in range(C):
                    maximum(l, 0, 0, c)
                negate_max(l, 0, 0)
                for n in range(1, C - 1):
                    store_y(l, n)
                mask(l, 0, 0)
                store_y(l, C - 1)
                if l == 0:
                    m_rest(1)

                step(l, 1, 1, finish=False, masking=False)
                if l == 0:
                    split_wa(1)
                for t in range(2, 6):
                    step(l, t, t % 2)
                with dve.Fori(3, T // 2 - 1) as u:
                    for b in range(2):
                        step(l, 2 * u + b, b)
                step(l, T - 2, 0)
                step(l, T - 1, 1, split=False)
                step(l, T, 0, scoring=False, split=False)
                if l < L - 1:
                    stage_x(l + 1, 0, 0, True)
                    stage_x(l + 1, 1, 1, True)
                    xT_rest(l + 1, 0, 0, True)
                    xT_rest(l + 1, 1, 1, True)
                    stage_x(l + 1, 2, 0, True)
                else:
                    last_epilogue(l, 1)
                    normalise(T - 2, 0, True)
                    dve.wait_ge(stats_ready, T)
                    aggregate(1)
                    normalise(T - 1, 1, True)

        @block.tensor
        def _(pe):
            def transpose_x(l, t, b, reuse):
                g = l * T + t
                pe.wait_ge(x_staged, g + 1)
                if reuse:
                    pe.wait_ge(xT_split, g - 1)
                for k in range(K):
                    mm = nc.tensor.transpose(tp[:, b, k * P:(k + 1) * P], x_stage[:, b, k * P:(k + 1) * P],
                                             ident[:])
                mm.then_inc(xT_ready, 1)

            def transpose_w(l):
                pe.wait_ge(w_loaded[l], 16)
                if l > 0:
                    pe.wait_ge(m_split, l)
                for h in range(2):
                    for m in range(K):
                        for k in range(K):
                            mm = nc.tensor.transpose(wT_bank[h][:, m * D + k * P:m * D + (k + 1) * P],
                                                     w_raw[:, l, k, h * D + m * P:h * D + (m + 1) * P], ident[:])
                    mm.then_inc(wT_ready, 1)

            def make_m(l):
                pe.wait_ge(wT_split, 2 * l + 2)
                (a_hi, a_lo), (b_hi, b_lo) = wT(0), wT(1)
                for k in range(K):
                    rows, dst = slice(k * P, (k + 1) * P), m_bank[l][:, k * D:(k + 1) * D]
                    for m in range(K):
                        nc.tensor.matmul(dst, a_hi[:, m, rows], b_hi[:, m, :], start=(m == 0), stop=False)
                        nc.tensor.matmul(dst, a_hi[:, m, rows], b_lo[:, m, :], start=False, stop=False)
                        mm = nc.tensor.matmul(dst, a_lo[:, m, rows], b_hi[:, m, :], start=False,
                                              stop=(m == K - 1))
                mm.then_inc(m_ready, 1)

            def project(l, t, i, reuse):
                g = l * T + t
                pe.wait_ge(xT_split, g + 1)
                if reuse:
                    pe.wait_ge(wh_split, g - XB + 1)
                if l > 0 and isinstance(t, int) and t == XB - 1:
                    pe.wait_ge(pv_sum_ready, g - t)
                for k in range(K):
                    nc.tensor.matmul(wh_bank[i], xT_hi[:, i, k, :], wa_hi[:, l, k, :], start=(k == 0), stop=False)
                    nc.tensor.matmul(wh_bank[i], xT_hi[:, i, k, :], wa_lo[:, l, k, :], start=False, stop=False)
                    mm = nc.tensor.matmul(wh_bank[i], xT_lo[:, i, k, :], wa_hi[:, l, k, :],
                                          start=False, stop=(k == K - 1))
                mm.then_inc(wh_ready, 1)

            def queries(l, n):
                pe.wait_ge(keys_hi_ready, l * T + (n + 1) * TPG)
                pe.wait_ge(keys_lo_ready, l * T + (n + 1) * TPG)
                if n >= 2:
                    pe.wait_ge(y_stored, K * (l * C + n - 1))
                cols = slice(n * BANK, (n + 1) * BANK)
                for f in range(K):
                    dst, rows = y_bank[n % 2][f], slice(f * P, (f + 1) * P)
                    for k in range(K):
                        nc.tensor.matmul(dst, m_hi[:, l, k, rows], keys_hi[:, k, cols], start=(k == 0), stop=False)
                        nc.tensor.matmul(dst, m_hi[:, l, k, rows], keys_lo[:, k, cols], start=False, stop=False)
                        mm = nc.tensor.matmul(dst, m_lo[:, l, k, rows], keys_hi[:, k, cols],
                                              start=False, stop=(k == K - 1))
                    mm.then_inc(y_ready, 1)

            def score(l, t, b, c):
                for k in range(K):
                    cols = slice(c * BANK, (c + 1) * BANK)
                    nc.tensor.matmul(scores[:, c, :], yT_hi[:, b, k, :], keys_hi[:, k, cols],
                                     start=(k == 0), stop=False)
                    nc.tensor.matmul(scores[:, c, :], yT_hi[:, b, k, :], keys_lo[:, k, cols],
                                     start=False, stop=False)
                    mm = nc.tensor.matmul(scores[:, c, :], yT_lo[:, b, k, :], keys_hi[:, k, cols],
                                          start=False, stop=(k == K - 1))
                mm.then_inc(scores_ready, 1)

            def transpose_probs(l, t, b, q):
                g = l * T + t
                pe.wait_ge(masked, C * g + q + 1)
                bank = BANK_OF_GROUP[q]
                if isinstance(t, int) and t == 0:
                    pe.wait_ge(y_stored, K * (l + 1) * C)
                    pe.wait_ge(m_split, 2)
                if q >= TP_BANKS:
                    pe.wait_ge(probsT_split, Q * g + q - TP_BANKS + 1)
                elif not (isinstance(t, int) and g == 0):
                    held = max(r for r in range(Q) if BANK_OF_GROUP[r] == bank)
                    pe.wait_ge(probsT_split, Q * (g - 1) + held + 1)
                for j in range(JB):
                    lhs = probs[:, b, (q * JB + j) * P:(q * JB + j + 1) * P]
                    mm = nc.tensor.transpose(tp[:, bank, j * P:(j + 1) * P], lhs, ident[:])
                mm.then_inc(probsT_ready, 1)

            def weigh(l, t, q):
                g = l * T + t
                pe.wait_ge(probsT_split, Q * g + q + 1)
                bank = pv_bank(t)
                if q == 0 and not (isinstance(t, int) and t in (0, T - 1)):
                    pe.wait_ge(pv_sum_ready, g)
                for j in range(JB):
                    first, final = q == 0 and j == 0, q == Q - 1 and j == JB - 1
                    rows = q * JB + j
                    hi, lo = (a[:, q, j * P:(j + 1) * P] for a in (probsT_hi, probsT_lo))

                    def with_lo():
                        nc.tensor.matmul(bank[:, 0:D], lo, wh[:, rows, 0:D], start=False, stop=False)

                    if isinstance(t, int) and t == T - 1:
                        nc.tensor.matmul(bank[:, 0:D], hi, wh[:, rows, 0:D], start=first, stop=False)
                        nc.tensor.matmul(bank[:, 0:D], hi, wh[:, rows, D:2 * D], start=False, stop=False)
                        mm = nc.tensor.matmul(bank[:, 0:D], lo, wh[:, rows, 0:D], start=False, stop=final)
                        continue
                    if final:
                        with_lo()
                    mm = nc.tensor.matmul(bank, hi, wh[:, rows, :], start=first, stop=final)
                    if not final:
                        with_lo()
                if q == Q - 1:
                    mm.then_inc(pv_ready, 1)

            def step(l, s, b):
                g = l * T + s
                pe.wait_ge(yT_split, g + 1)
                for c in range(C):
                    if c == C - 1:
                        transpose_probs(l, s - 1, 1 - b, 0)
                        transpose_probs(l, s - 1, 1 - b, 1)
                    pe.wait_ge(probs_ready, C * (g - 1) + c + 1)
                    score(l, s, b, c)
                value_rest(l, s - 1, 1 - b, s)

            def value_rest(l, t, b, s):
                transpose_probs(l, t, b, 2)
                weigh(l, t, 0)
                transpose_probs(l, t, b, 3)
                weigh(l, t, 1)
                weigh(l, t, 2)
                if isinstance(s, int) and s == T - 1:
                    transpose_probs(l, T - 1, 1, 0)
                    transpose_probs(l, T - 1, 1, 1)
                if isinstance(s, int) and s == T and l < L - 1:
                    transpose_x(l + 1, 0, 0, True)
                    transpose_x(l + 1, 1, 1, True)
                weigh(l, t, 3)

            def keys_step(l, t, i):
                transpose_x(l, t + 2, i % 2, True)
                project(l, t, i, l > 0 or not (isinstance(t, int) and t < XB))

            pe.wait_ge(consts_ready, 2)
            for _ in range(WARM_UP):
                nc.tensor.transpose(pv[:, 0:P], ident[:], ident[:])
            transpose_x(0, 0, 0, False)
            transpose_x(0, 1, 1, False)
            transpose_w(0)
            pe.wait_ge(wa_split, 1)
            for l in range(L):
                for t in range(XB):
                    keys_step(l, t, t)
                if l == 0:
                    make_m(0)
                with pe.Fori(1, T // XB - 1) as u:
                    for i in range(XB):
                        keys_step(l, XB * u + i, i)
                keys_step(l, T - 4, 0)
                keys_step(l, T - 3, 1)
                project(l, T - 2, 2, True)
                project(l, T - 1, 3, True)
                if l == 0:
                    transpose_w(1)

                pe.wait_ge(m_split, l + 1)
                queries(l, 0)
                if l == 0:
                    pe.wait_ge(wT_split, 4)
                queries(l, 1)
                pe.wait_ge(yT_split, l * T + 1)
                for c in range(C):
                    if c == 0:
                        pe.wait_ge(wh_split, (l + 1) * T)
                    pe.wait_ge(keys_hi_ready, l * T + (c + 1) * TPG)
                    pe.wait_ge(keys_lo_ready, l * T + (c + 1) * TPG)
                    score(l, 0, 0, c)
                for n in range(2, C):
                    queries(l, n)
                if l == 0:
                    pe.wait_ge(y_stored, K * (C - 1))
                    make_m(1)

                step(l, 1, 1)
                with pe.Fori(1, T // 2 - 1) as u:
                    for b in range(2):
                        step(l, 2 * u + b, b)
                step(l, T - 2, 0)
                step(l, T - 1, 1)
                value_rest(l, T - 1, 1, T)


_INS = ['x', 'adj', 'L0_gnn_W_stack']
_OUTS = [((2048, 256), 'float32')]


def kernel(**inputs):
    import numpy as _np
    import concourse.bacc as _bacc
    from concourse import mybir as _mybir
    from concourse.bass_utils import run_bass_kernel_spmd as _run

    nc = _bacc.Bacc("TRN2", target_bir_lowering=False, num_devices=1)
    arrays, args = {}, []
    for name in _INS:
        a = _np.ascontiguousarray(inputs[name])
        arrays[f"in_{name}_dram"] = a
        args.append(nc.dram_tensor(f"in_{name}_dram", a.shape, _mybir.dt.from_np(a.dtype), kind="ExternalInput").ap())
    for i, (shape, dtype) in enumerate(_OUTS):
        dt = _mybir.dt.from_np(_np.dtype(dtype))
        args.append(nc.dram_tensor(f"out_{i}_dram", shape, dt, kind="ExternalOutput").ap())
    gat_resnorm_kernel(nc, *args)
    r = _run(nc, [arrays], core_ids=[0])
    got = tuple(r.results[0][f"out_{i}_dram"] for i in range(len(_OUTS)))
    return got[0]
```
